# Optimizing a Trainium2 kernel written in Bass

```python
import numpy as np
import jax
import jax.numpy as jnp

def _softmax(x, axis=-1):
    return jax.nn.softmax(x, axis=axis)

def _gelu(x):
    return jax.nn.gelu(x, approximate=True)

def _silu(x):
    return jax.nn.silu(x)

def _sigmoid(x):
    return jax.nn.sigmoid(x)

def _layernorm(x, axis=-1, eps=1e-05):
    m = jnp.mean(x, axis=axis, keepdims=True)
    v = jnp.var(x, axis=axis, keepdims=True)
    return (x - m) / jnp.sqrt(v + eps)

def _scatter_add(tgt, idx, src, axis=0):
    return tgt.at[idx].add(src)

def _segment_sum(src, seg, n):
    return jax.ops.segment_sum(src, seg, n)
kernel_name = 'mk_macaron_d1_jaxref_r8_a99173'

def setup_inputs(seed: int=0):
    np.random.seed(seed)
    _w = jnp.asarray

    def _L0_attn_setup():
        import jax, jax.numpy as jnp
        import numpy as np
        WIDTH = 128
        NUM_HEADS = 16
        HEAD_DIM = WIDTH // NUM_HEADS
        WINDOW = 32
        BATCH = 2
        SEQ = 256
        _MIN_LOGITS_VALUE = -1e+30
        key = jax.random.key(seed)
        ks = jax.random.split(key, 6)
        std = 1.0 / np.sqrt(WIDTH)
        x = jax.random.normal(ks[0], (BATCH, SEQ, WIDTH), dtype=jnp.float32)
        Wq = jax.random.normal(ks[1], (WIDTH, WIDTH), dtype=jnp.float32) * std
        Wk = jax.random.normal(ks[2], (HEAD_DIM, WIDTH), dtype=jnp.float32) * std
        Wv = jax.random.normal(ks[3], (HEAD_DIM, WIDTH), dtype=jnp.float32) * std
        Wf = jax.random.normal(ks[4], (WIDTH, WIDTH), dtype=jnp.float32) * std
        bf = jnp.zeros((WIDTH,), dtype=jnp.float32)
        return {'x': x, 'Wq': Wq, 'Wk': Wk, 'Wv': Wv, 'Wf': Wf, 'bf': bf}
    _L0_attn_in = _L0_attn_setup()

    def _L0_ffn_setup():
        import jax, jax.numpy as jnp
        import numpy as np
        H = 128
        M = 64
        E = 16
        TOP_K = 4
        N_GROUP = 4
        TOPK_GROUP = 2
        SCALE = 2.5
        B, S = (2, 128)

        def _gate(x2d, gate_kernel, gate_bias):
            n = x2d.shape[0]
            logits = jnp.dot(x2d.astype(jnp.float32), gate_kernel.astype(jnp.float32))
            scores = jax.nn.sigmoid(logits)
            scores_for_choice = scores + gate_bias
            group_scores = scores_for_choice.reshape(n, N_GROUP, E // N_GROUP)
            top2 = jax.lax.top_k(group_scores, k=2)[0]
            group_sum = jnp.sum(top2, axis=-1)
            group_idx = jax.lax.top_k(group_sum, k=TOPK_GROUP)[1]
            group_mask = jnp.zeros_like(group_sum).at[jnp.arange(n)[:, None], group_idx].set(1.0)
            score_mask = jnp.repeat(group_mask[:, :, None], E // N_GROUP, axis=2).reshape(n, E)
            masked_scores = jnp.where(score_mask > 0, scores_for_choice, 0.0)
            topk_weight, topk_idx = jax.lax.top_k(masked_scores, k=TOP_K)
            topk_weight = topk_weight / (jnp.sum(topk_weight, axis=-1, keepdims=True) + 1e-20)
            topk_weight = topk_weight * SCALE
            return (topk_idx, topk_weight)
        key = jax.random.key(seed)
        ks = jax.random.split(key, 9)
        sc_h = 1.0 / np.sqrt(H)
        sc_m = 1.0 / np.sqrt(M)
        return {'hidden_states': jax.random.normal(ks[0], (B, S, H), jnp.float32), 'gate_kernel': jax.random.normal(ks[1], (H, E), jnp.float32) * sc_h, 'gate_bias': jax.random.normal(ks[2], (E,), jnp.float32) * 0.01, 'w_gate': jax.random.normal(ks[3], (E, H, M), jnp.float32) * sc_h, 'w_up': jax.random.normal(ks[4], (E, H, M), jnp.float32) * sc_h, 'w_down': jax.random.normal(ks[5], (E, M, H), jnp.float32) * sc_m, 'sw_gate': jax.random.normal(ks[6], (H, 2 * M), jnp.float32) * sc_h, 'sw_up': jax.random.normal(ks[7], (H, 2 * M), jnp.float32) * sc_h, 'sw_down': jax.random.normal(ks[8], (2 * M, H), jnp.float32) * (1.0 / np.sqrt(2 * M))}
    _L0_ffn_in = _L0_ffn_setup()
    _d = {'L0_attn_x': _L0_attn_in['x'], 'L0_attn_Wq': _L0_attn_in['Wq'], 'L0_attn_Wk': _L0_attn_in['Wk'], 'L0_attn_Wv': _L0_attn_in['Wv'], 'L0_attn_Wf': _L0_attn_in['Wf'], 'L0_attn_bf': _L0_attn_in['bf'], 'L0_ffn_gate_kernel': _L0_ffn_in['gate_kernel'], 'L0_ffn_gate_bias': _L0_ffn_in['gate_bias'], 'L0_ffn_w_gate': _L0_ffn_in['w_gate'], 'L0_ffn_w_up': _L0_ffn_in['w_up'], 'L0_ffn_w_down': _L0_ffn_in['w_down'], 'L0_ffn_sw_gate': _L0_ffn_in['sw_gate'], 'L0_ffn_sw_up': _L0_ffn_in['sw_up'], 'L0_ffn_sw_down': _L0_ffn_in['sw_down']}
    _x0 = _d['L0_attn_x']
    _d['L0_attn_x'] = jax.random.normal(jax.random.fold_in(jax.random.key(seed), 1), (4, 512, 128), dtype=_x0.dtype)
    del _x0
    return _d

def reference(L0_attn_x, L0_attn_Wq, L0_attn_Wk, L0_attn_Wv, L0_attn_Wf, L0_attn_bf, L0_ffn_gate_kernel, L0_ffn_gate_bias, L0_ffn_w_gate, L0_ffn_w_up, L0_ffn_w_down, L0_ffn_sw_gate, L0_ffn_sw_up, L0_ffn_sw_down):

    def _L0_attn_ref(x, Wq, Wk, Wv, Wf, bf):
        import jax, jax.numpy as jnp
        import numpy as np
        WIDTH = 128
        NUM_HEADS = 16
        HEAD_DIM = WIDTH // NUM_HEADS
        WINDOW = 32
        BATCH = 2
        SEQ = 256
        _MIN_LOGITS_VALUE = -1e+30
        b, t, _ = x.shape
        q = (x @ Wq.T).reshape(b, t, NUM_HEADS, HEAD_DIM)
        k = x @ Wk.T
        v = x @ Wv.T
        scale = 1.0 / np.sqrt(HEAD_DIM)
        logits = jnp.einsum('btnh,bsh->bnts', q, k) * scale
        pos = jnp.arange(t)
        mask = jnp.abs(pos[:, None] - pos[None, :]) <= WINDOW
        masked = jnp.where(mask[None, None, :, :], logits, _MIN_LOGITS_VALUE)
        probs = jax.nn.softmax(masked.astype(jnp.float32), axis=-1).astype(logits.dtype)
        out = jnp.einsum('bnts,bsh->btnh', probs, v).reshape(b, t, WIDTH)
        return out @ Wf.T + bf

    def _L0_ffn_ref(hidden_states, gate_kernel, gate_bias, w_gate, w_up, w_down, sw_gate, sw_up, sw_down):
        import jax, jax.numpy as jnp
        import numpy as np
        H = 128
        M = 64
        E = 16
        TOP_K = 4
        N_GROUP = 4
        TOPK_GROUP = 2
        SCALE = 2.5
        B, S = (2, 128)

        def _gate(x2d, gate_kernel, gate_bias):
            n = x2d.shape[0]
            logits = jnp.dot(x2d.astype(jnp.float32), gate_kernel.astype(jnp.float32))
            scores = jax.nn.sigmoid(logits)
            scores_for_choice = scores + gate_bias
            group_scores = scores_for_choice.reshape(n, N_GROUP, E // N_GROUP)
            top2 = jax.lax.top_k(group_scores, k=2)[0]
            group_sum = jnp.sum(top2, axis=-1)
            group_idx = jax.lax.top_k(group_sum, k=TOPK_GROUP)[1]
            group_mask = jnp.zeros_like(group_sum).at[jnp.arange(n)[:, None], group_idx].set(1.0)
            score_mask = jnp.repeat(group_mask[:, :, None], E // N_GROUP, axis=2).reshape(n, E)
            masked_scores = jnp.where(score_mask > 0, scores_for_choice, 0.0)
            topk_weight, topk_idx = jax.lax.top_k(masked_scores, k=TOP_K)
            topk_weight = topk_weight / (jnp.sum(topk_weight, axis=-1, keepdims=True) + 1e-20)
            topk_weight = topk_weight * SCALE
            return (topk_idx, topk_weight)
        orig_shape = hidden_states.shape
        x = hidden_states.reshape(-1, orig_shape[-1])
        topk_idx, topk_weight = _gate(x, gate_kernel, gate_bias)
        onehot = (topk_idx[:, :, None] == jnp.arange(E)[None, None, :]).astype(topk_weight.dtype)
        combine = jnp.einsum('nke,nk->ne', onehot, topk_weight)
        g = jnp.einsum('nh,ehm->enm', x, w_gate)
        u = jnp.einsum('nh,ehm->enm', x, w_up)
        inter = jax.nn.silu(g) * u
        y_e = jnp.einsum('enm,emh->enh', inter, w_down)
        y = jnp.einsum('ne,enh->nh', combine, y_e)
        shared = jnp.dot(jax.nn.silu(jnp.dot(x, sw_gate)) * jnp.dot(x, sw_up), sw_down)
        return (y + shared).reshape(orig_shape)
    x = L0_attn_x
    x = x + 0.5 * _L0_ffn_ref(_layernorm(x, axis=-1), L0_ffn_gate_kernel, L0_ffn_gate_bias, L0_ffn_w_gate, L0_ffn_w_up, L0_ffn_w_down, L0_ffn_sw_gate, L0_ffn_sw_up, L0_ffn_sw_down)
    x = x + _L0_attn_ref(_layernorm(x, axis=-1), L0_attn_Wq, L0_attn_Wk, L0_attn_Wv, L0_attn_Wf, L0_attn_bf)
    x = x + 0.5 * _L0_ffn_ref(_layernorm(x, axis=-1), L0_ffn_gate_kernel, L0_ffn_gate_bias, L0_ffn_w_gate, L0_ffn_w_up, L0_ffn_w_down, L0_ffn_sw_gate, L0_ffn_sw_up, L0_ffn_sw_down)
    return x

_drawn_inputs = setup_inputs


def setup_inputs(seed=0):
    import zlib

    import numpy as np

    out = dict(_drawn_inputs(seed))
    spreads = {'L0_attn_bf': (0.0, 0.1)}
    factors = {}
    for name, (base, spread) in spreads.items():
        noise = np.random.default_rng([zlib.crc32(name.encode()), seed]).standard_normal(out[name].shape)
        drawn = base * np.exp(spread * noise) if base else spread * noise
        out[name] = jnp.asarray(drawn.astype(out[name].dtype))
    for name, factor in factors.items():
        out[name] = (out[name] * factor).astype(out[name].dtype)
    return out
```

```python
from contextlib import ExitStack

import concourse.bass as bass
from concourse import mybir

ALU = mybir.AluOpType
ACT = mybir.ActivationFunctionType
AX = mybir.AxisListType
F32 = mybir.dt.float32
F32R = mybir.dt.float32r
BF16 = mybir.dt.bfloat16

P = 128
NB, SEQ, D = 4, 512, 128
NT = SEQ // P
E, M = 16, 64
CH = E * M // P + 1
NP2 = CH - 1
GROUPS, TOP_GROUPS, TOP_K, ROUTE_SCALE = 4, 2, 4, 2.5
HD, WINDOW = 8, 32
QB = 64
NBLK = SEQ // QB
EPS = 1e-5
UNITS = 2 * NB
LAG = 2

TICKS = NBLK + 4
CHUNK_TICKS = [0, 1, 2, 4, 5, 7, 8, 10, 11]


def key_start(i):
    return min(max(QB * i - WINDOW, 0), SEQ - P)


def mask_kind(i):
    return 0 if i == 0 else 2 if i == NBLK - 1 else 1


def macaron(nc, x, wg, wu, wd, gk, gbias, wq, wk, wv, wf, bf, ident_in, mask_in, sel_in, tri_in, beta_in, out):
    ctx = ExitStack()
    with ctx:
        def sb(name, shape, dt=F32):
            return ctx.enter_context(nc.sbuf_tensor(name, shape, dt))

        def ps(name, shape):
            return ctx.enter_context(nc.psum_tensor(name, shape, F32))

        def sem(name):
            return ctx.enter_context(nc.semaphore(name))

        X = sb("X", [P, UNITS, NT, D])
        wg_raw = sb("wg_raw", [P, CH * P])
        wu_raw = sb("wu_raw", [P, CH * P])
        wg_hi, wg_lo = sb("wg_hi", [P, CH * P], F32R), sb("wg_lo", [P, CH * P], F32R)
        wu_hi, wu_lo = sb("wu_hi", [P, CH * P], F32R), sb("wu_lo", [P, CH * P], F32R)
        wd_sb = sb("wd_sb", [P, CH, D])
        gk_raw = sb("gk_raw", [P, E])
        gk_hi, gk_lo = sb("gk_hi", [P, E], F32R), sb("gk_lo", [P, E], F32R)
        gbias_sb = sb("gbias_sb", [P, E])
        wq_raw = sb("wq_raw", [P, D])
        wq_scaled = sb("wq_scaled", [P, D])
        wk_raw = sb("wk_raw", [P, HD])
        wv_raw = sb("wv_raw", [P, HD])
        wq_hi, wq_lo = sb("wq_hi", [P, 4, P], F32R), sb("wq_lo", [P, 4, P], F32R)
        wk_hi, wk_lo = sb("wk_hi", [P, P], F32R), sb("wk_lo", [P, P], F32R)
        wv_hi, wv_lo = sb("wv_hi", [P, HD], F32R), sb("wv_lo", [P, HD], F32R)
        wf_sb = sb("wf_sb", [P // 2, 2, D])
        bf_sb = sb("bf_sb", [1, D])
        ones_row = sb("ones_row", [1, P])
        ident = sb("ident", [P, P])
        ident_bf = sb("ident_bf", [P, P], BF16)
        mask_raw = sb("mask_raw", [P, 3, P])
        mask = sb("mask", [P, 3, P], BF16)
        sel_raw = sb("sel_raw", [P, NP2, P])
        sel = sb("sel", [P, NP2, P], F32R)
        tri = sb("tri", [P, GROUPS, GROUPS])
        beta = sb("beta", [P, 2])
        half = sb("half", [P, NT])
        eps = sb("eps", [P, NT])
        pause = sb("pause", [P, 1])

        stats = sb("stats", [P, NT, 6])
        mv = sb("mv", [P, NT, 2])
        var_eps = sb("var_eps", [P, NT])
        rstd = sb("rstd", [P, NT])
        xn = sb("xn", [P, NT, D])
        xt_next_hi, xt_next_lo = sb("xt_next_hi", [P, SEQ], F32R), sb("xt_next_lo", [P, SEQ], F32R)
        xt_hi, xt_lo = sb("xt_hi", [P, SEQ], F32R), sb("xt_lo", [P, SEQ], F32R)
        xa_hi, xa_lo = sb("xa_hi", [P, SEQ], F32R), sb("xa_lo", [P, SEQ], F32R)
        r_exp = sb("r_exp", [P, NT, E])
        r_den = sb("r_den", [P, NT, E])
        r_score = sb("r_score", [P, NT, E])
        r_choice = sb("r_choice", [P, NT, E])
        r_max = sb("r_max", [P, NT * GROUPS, 2])
        r_min = sb("r_min", [P, NT * GROUPS, 2])
        r_top1 = sb("r_top1", [P, NT * GROUPS])
        r_mid = sb("r_mid", [P, NT * GROUPS])
        r_low = sb("r_low", [P, NT * GROUPS])
        r_top2 = sb("r_top2", [P, NT * GROUPS])
        r_group = sb("r_group", [P, NT, GROUPS])
        r_gt = sb("r_gt", [P, NT, GROUPS, GROUPS])
        r_eq = sb("r_eq", [P, NT, GROUPS, GROUPS])
        r_eq_tri = sb("r_eq_tri", [P, NT, GROUPS, GROUPS])
        r_before = sb("r_before", [P, NT, GROUPS, GROUPS])
        r_rank = sb("r_rank", [P, NT * GROUPS])
        r_gmask = sb("r_gmask", [P, NT * GROUPS])
        r_masked = sb("r_masked", [P, NT, E])
        r_top8 = sb("r_top8", [P, NT, 8])
        r_above = sb("r_above", [P, NT, E])
        r_n_above = sb("r_n_above", [P, NT])
        r_room = sb("r_room", [P, NT])
        scan_a = sb("scan_a", [P, NT, 8 + E])
        scan_b = sb("scan_b", [P, NT, 8 + E])
        r_tie = sb("r_tie", [P, NT, E])
        r_fits = sb("r_fits", [P, NT, E])
        r_tie_in = sb("r_tie_in", [P, NT, E])
        r_pick = sb("r_pick", [P, NT, E])
        r_w = sb("r_w", [P, NT, E])
        r_sum = sb("r_sum", [P, NT])
        r_sum_eps = sb("r_sum_eps", [P, NT])
        r_inv = sb("r_inv", [P, NT])
        r_comb = sb("r_comb", [P, NT, E])
        comb = sb("comb", [P, NT, P])
        comb_t = sb("comb_t", [P, SEQ], F32R)

        th = sb("th", [P, SEQ])
        sg = sb("sg", [P, SEQ])
        gu = sb("gu", [P, SEQ])
        hid = sb("hid", [P, 2, SEQ])
        y_sb = sb("y_sb", [P, SEQ])

        qk_hi = sb("qk_hi", [P, 2, SEQ], F32R)
        q_rep = sb("q_rep", [P, 2, NBLK, 2, QB], F32R)
        k_diag = sb("k_diag", [P, 4, SEQ], F32R)
        v_one = sb("v_one", [P, NBLK, HD + 1])
        neg_max = sb("neg_max", [P, 8])
        prob = sb("prob", [P, 8, P])
        prob_t = sb("prob_t", [P, 8, P])
        o_inv = sb("o_inv", [P, 8])
        o_norm = sb("o_norm", [P, 8, HD])
        o_t = sb("o_t", [P // 2, 2, SEQ])

        pG, pU, pA, pY = ps("pG", [P, SEQ]), ps("pU", [P, SEQ]), ps("pA", [P, SEQ]), ps("pY", [P, SEQ])
        pS0, pS1, pT, pO = ps("pS0", [P, SEQ]), ps("pS1", [P, SEQ]), ps("pT", [P, SEQ]), ps("pO", [P, SEQ])
        O_T = 256
        q_banks = [pS1, pT, pO, pS0]
        k_bank, v_bank = pS1, pT

        x_in = [sem(f"x_in{b}") for b in range(NB)]
        const_in, wg_in, wu_in, wd_in, attn_w_in, route_in, out_done = (
            sem(n) for n in ("const_in", "wg_in", "wu_in", "wd_in", "attn_w_in", "route_in", "out_done"))
        zeroed, consts_ready = sem("zeroed"), sem("consts_ready")
        w_hi_done, w_lo_done = sem("w_hi_done"), sem("w_lo_done")
        wq_scaled_done, attn_hi_done, attn_lo_done = sem("wq_scaled_done"), sem("attn_hi_done"), sem("attn_lo_done")
        stats_done, mv_done, eps_done, rstd_done, xn_done = (
            sem(n) for n in ("stats_done", "mv_done", "eps_done", "rstd_done", "xn_done"))
        astats_done, amv_done, aeps_done, arstd_done, axn_done = (
            sem(n) for n in ("astats_done", "amv_done", "aeps_done", "arstd_done", "axn_done"))
        xt_psum, xt_hi_done, xt_lo_done = sem("xt_psum"), sem("xt_hi_done"), sem("xt_lo_done")
        xa_psum, xa_hi_done, xa_lo_done = sem("xa_psum"), sem("xa_hi_done"), sem("xa_lo_done")
        logits_psum, gate_exp_done, route_step, comb_done = (
            sem(n) for n in ("logits_psum", "gate_exp_done", "route_step", "comb_done"))
        comb_psum, comb_t_done = sem("comb_psum"), sem("comb_t_done")
        xt_moved_hi, xt_moved_lo = sem("xt_moved_hi"), sem("xt_moved_lo")
        g_psum, u_psum, c_psum = sem("g_psum"), sem("u_psum"), sem("c_psum")
        tanh_done, sg_done, gu_done, hid_done, down_done = (
            sem(n) for n in ("tanh_done", "sg_done", "gu_done", "hid_done", "down_done"))
        y_copied, y_back, x_added = sem("y_copied"), sem("y_back"), sem("x_added")
        qk_psum, qk_hi_done, qk_done, v_psum, v_done = (
            sem(n) for n in ("qk_psum", "qk_hi_done", "qk_done", "v_psum", "v_done"))
        s_psum, max_done, exp_done, t_psum, t_copied = (
            sem(n) for n in ("s_psum", "max_done", "exp_done", "t_psum", "t_copied"))
        o_psum, o_inv_done, o_norm_done, ot_psum, ot_copied = (
            sem(n) for n in ("o_psum", "o_inv_done", "o_norm_done", "ot_psum", "ot_copied"))
        attn_psum, attn_added = sem("attn_psum"), sem("attn_added")

        WGP = 3
        WPC = CH * P // WGP
        ROUTE_STEPS = 34

        def wait(eng, s, per, index, k):
            n = index * per + k
            if not isinstance(n, int) or n > 0:
                eng.wait_ge(s, n)

        def wait_apart(eng, s, per, index, k):
            if isinstance(index, int):
                wait(eng, s, per, index, k)
            else:
                n = eng.snap(index * per + k)
                eng.wait_ge(zeroed, 8)
                eng.wait_ge(s, n)

        def schedule(attn):
            if attn:
                return [(t, CHUNK_TICKS.index(t) if t in CHUNK_TICKS else None) for t in range(TICKS)]
            return [(t, t) for t in range(CH)]

        def q_heads(w, c):
            h0 = 8 * (c % 2) + 4 * (c // 2)
            return w[:, HD * h0:HD * (h0 + 4)].rearrange("p (j d) -> p j d", d=HD).unsqueeze(2)\
                .to_broadcast([P, 4, 4, HD])

        def units(eng, unit):
            unit(0, False, False, False)
            unit(1, False, True, False)
            unit(2, True, True, False)
            with eng.Fori(3, 5) as u:
                unit(u, True, True, False)
            unit(5, True, False, False)
            unit(6, False, False, False)
            unit(7, False, False, True)

        block = ctx.enter_context(nc.Block())

        @block.sync
        def _(sp):
            x_t = x.rearrange("(u t p) d -> u p t d", p=P, t=NT)
            out_t = out.rearrange("(u t p) d -> u p t d", p=P, t=NT)
            sp.dma_start(X[:, 0], x_t[0]).then_inc(x_in[0], 16)
            sp.dma_start(ident[:], ident_in).then_inc(const_in, 16)
            sp.dma_start(tri[:], tri_in).then_inc(const_in, 16)
            sp.dma_start(gk_raw[:], gk).then_inc(route_in, 16)
            sp.dma_start(gbias_sb[:], gbias).then_inc(route_in, 16)
            sp.dma_start(wg_raw[:], wg).then_inc(wg_in, 16)
            sp.dma_start(wu_raw[:], wu).then_inc(wu_in, 16)
            sp.dma_start(sel_raw[:], sel_in).then_inc(const_in, 16)
            sp.dma_start(wd_sb[:], wd).then_inc(wd_in, 16)
            for b in range(1, NB):
                sp.dma_start(X[:, b], x_t[b]).then_inc(x_in[b], 16)
            sp.dma_start(mask_raw[:], mask_in).then_inc(attn_w_in, 16)
            sp.dma_start(beta[:], beta_in).then_inc(attn_w_in, 16)
            sp.dma_start(wq_raw[:], wq).then_inc(attn_w_in, 16)
            sp.dma_start(wk_raw[:], wk).then_inc(attn_w_in, 16)
            sp.dma_start(wv_raw[:], wv).then_inc(attn_w_in, 16)
            sp.dma_start(wf_sb[:], wf).then_inc(attn_w_in, 16)
            sp.dma_start(bf_sb[:], bf).then_inc(attn_w_in, 16)
            for u in range(NB, UNITS):
                sp.wait_ge(x_added, u + 1)
                sp.dma_start(out_t[u - NB], X[:, u]).then_inc(out_done, 16)
            sp.wait_ge(out_done, 16 * NB)

        @block.gpsimd
        def _(pool):
            pool.memset(half[:], -0.5).then_inc(zeroed, 1)
            pool.memset(eps[:], EPS).then_inc(zeroed, 1)
            pool.memset(ones_row[:], 1.0).then_inc(zeroed, 1)
            pool.memset(comb[:], 0.0).then_inc(zeroed, 1)
            pool.memset(scan_a[:], 0.0).then_inc(zeroed, 1)
            pool.memset(scan_b[:], 0.0).then_inc(zeroed, 1)
            pool.memset(v_one[:], 1.0).then_inc(zeroed, 1)
            pool.memset(k_diag[:].bitcast(F32), 0.0).then_inc(zeroed, 1)

            def rstd_of(mv_sem, eps_sem, rstd_sem, run):
                wait(pool, mv_sem, NT, run, NT)
                pool.tensor_tensor(var_eps[:], mv[:, :, 1], eps[:], ALU.add).then_inc(eps_sem, 1)
                wait(pool, eps_sem, 1, run, 1)
                pool.tensor_tensor(rstd[:], var_eps[:], half[:], ALU.pow).then_inc(rstd_sem, 1)

            pool.wait_ge(zeroed, 2)
            rstd_of(mv_done, eps_done, rstd_done, 0)

            def unit(u, attn, next_attn, last):
                if not last:
                    rstd_of(mv_done, eps_done, rstd_done, u + 1)
                if next_attn:
                    rstd_of(amv_done, aeps_done, arstd_done, u - 1)

            units(pool, unit)

        @block.scalar
        def _(act):
            def next_x(run):
                wait(act, xt_psum, 1, run, 1)
                act.activation(xt_next_hi[:], pA[:], ACT.Copy).then_inc(xt_hi_done, 1)

            def gate_exp(run):
                wait(act, logits_psum, 1, run, 1)
                act.activation(r_exp[:], pA[:, 0:NT * E].rearrange("p (t e) -> p t e", t=NT), ACT.Exp,
                               scale=-1.0).then_inc(gate_exp_done, 1)

            act.wait_ge(route_in, 32)
            act.activation(gk_hi[:], gk_raw[:], ACT.Copy).then_inc(w_hi_done, 1)
            next_x(0)
            for n in range(WGP):
                cols = slice(n * WPC, (n + 1) * WPC)
                if n == 0:
                    act.wait_ge(wg_in, 16)
                act.activation(wg_hi[:, cols], wg_raw[:, cols], ACT.Copy).then_inc(w_hi_done, 1)
                if n == 0:
                    act.wait_ge(wu_in, 16)
                act.activation(wu_hi[:, cols], wu_raw[:, cols], ACT.Copy).then_inc(w_hi_done, 1)
                if n == 0:
                    gate_exp(0)
            act.wait_ge(const_in, 48)
            act.activation(sel[:], sel_raw[:], ACT.Copy).then_inc(consts_ready, 1)
            act.wait_ge(attn_w_in, 7 * 16)
            act.activation(ident_bf[:], ident[:], ACT.Copy).then_inc(consts_ready, 1)
            act.activation(mask[:], mask_raw[:], ACT.Copy).then_inc(consts_ready, 1)
            act.mul(wq_scaled[:], wq_raw[:], float(HD) ** -0.5).then_inc(wq_scaled_done, 1)
            act.wait_ge(wq_scaled_done, 1)
            for c in range(4):
                act.activation(wq_hi[:, c, :].rearrange("p (j r d) -> p j r d", j=4, r=4), q_heads(wq_scaled, c),
                               ACT.Copy).then_inc(attn_hi_done, 1)
            act.activation(wk_hi[:].rearrange("p (r d) -> p r d", d=HD),
                           wk_raw[:].unsqueeze(1).to_broadcast([P, P // HD, HD]), ACT.Copy).then_inc(attn_hi_done, 1)
            act.activation(wv_hi[:], wv_raw[:], ACT.Copy).then_inc(attn_hi_done, 1)

            def unit(u, attn, next_attn, last):
                a = u - LAG
                wait(act, xt_hi_done, 1, u, 1)
                wait(act, u_psum, CH, u, 0)
                act.activation(xt_hi[:], xt_next_hi[:].bitcast(F32), ACT.Copy).then_inc(xt_moved_hi, 1)
                wait(act, comb_psum, 1, u, 1)
                act.activation(comb_t[:], pA[:], ACT.Copy).then_inc(comb_t_done, 1)
                for t, e in schedule(attn):
                    if attn and t == 0:
                        if isinstance(u, int):
                            act.wait_ge(zeroed, 8)
                        for c in range(5):
                            wait(act, qk_psum, 5, a, c + 1)
                            if c < 2:
                                wait(act, qk_done, 8, a, 0)
                            else:
                                wait(act, qk_done, 8, a, c - 1)
                            act.activation(qk_hi[:, c % 2, :], (q_banks + [k_bank])[c][:], ACT.Copy)\
                               .then_inc(qk_hi_done, 1)
                            if e is not None and c == 1:
                                wait(act, g_psum, CH, u, 1)
                                act.activation(th[:], pG[:], ACT.Tanh, scale=0.5).then_inc(tanh_done, 1)
                        wait(act, v_psum, 1, a, 1)
                        act.activation(v_one[:, :, 0:HD], v_bank[:, 0:NBLK * HD].rearrange("p (i d) -> p i d", d=HD),
                                       ACT.Copy).then_inc(v_done, 1)
                    if attn and t >= 3 and t - 3 < NBLK:
                        i = t - 3
                        wait(act, ot_psum, NBLK, a, i + 1)
                        act.activation(o_t[:, :, QB * i:QB * (i + 1)],
                                       pO[0:P // 2, O_T:O_T + P].rearrange("p (c q) -> p c q", c=2),
                                       ACT.Copy).then_inc(ot_copied, 1)
                    if attn and 2 <= t < NBLK + 2:
                        i = t - 2
                        wait(act, t_psum, 2 * NBLK, a, 2 * i + 1)
                        wait(act, o_psum, NBLK, a, i)
                        act.activation(prob_t[:, 0:4, :], pT[:].rearrange("p (s k) -> p s k", s=4),
                                       ACT.Copy).then_inc(t_copied, 1)
                    if e is not None and not (attn and t == 0):
                        wait(act, g_psum, CH, u, e + 1)
                        act.activation(th[:], pG[:], ACT.Tanh, scale=0.5).then_inc(tanh_done, 1)
                    if attn and 2 <= t < NBLK + 2:
                        i = t - 2
                        wait(act, t_psum, 2 * NBLK, a, 2 * i + 2)
                        act.activation(prob_t[:, 4:8, :], pT[:].rearrange("p (s k) -> p s k", s=4),
                                       ACT.Copy).then_inc(t_copied, 1)
                    if e == 0 and not (isinstance(u, int) and u == 0):
                        wait(act, down_done, CH, u, 0)
                        act.activation(y_sb[:], pY[:], ACT.Copy).then_inc(y_copied, 1)
                    if e == 2 and not last:
                        next_x(u + 1)
                    if e == 3 and not last:
                        gate_exp(u + 1)
                    if e == 5 and next_attn:
                        wait(act, xa_psum, 1, u - 1, 1)
                        act.activation(xa_hi[:], pA[:], ACT.Copy).then_inc(xa_hi_done, 1)
                    if attn and 1 <= t < NBLK + 1:
                        i = t - 1
                        wait(act, max_done, NBLK, a, i + 1)
                        wait(act, t_psum, 2 * NBLK, a, 2 * i)
                        for s in range(8):
                            ins = act.activation(prob[:, s, :], (pS0, pS1)[s // 4][:, P * (s % 4):P * (s % 4 + 1)],
                                                 ACT.Exp, bias=neg_max[:, s:s + 1])
                        ins.then_inc(exp_done, 1)

            units(act, unit)
            act.wait_ge(down_done, CH * UNITS)
            act.activation(y_sb[:], pY[:], ACT.Copy).then_inc(y_copied, 1)

        @block.vector
        def _(dve):
            def wait_by_memset(s, per, index, k):
                wait(dve, s, per, index, k)
                if not isinstance(index, int):
                    dve.memset(pause[:], 0.0)

            def layernorm(slot, sems, run):
                s_stats, s_mv, s_rstd, s_xn = sems
                for t in range(NT):
                    dve.bn_stats(stats[:, t, :], X[:, slot, t, :]).then_inc(s_stats, 1)
                wait_by_memset(s_stats, NT, run, NT)
                for t in range(NT):
                    dve.bn_aggr(mv[:, t, :], stats[:, t, :]).then_inc(s_mv, 1)

            def normalize(slot, sems, run):
                s_stats, s_mv, s_rstd, s_xn = sems
                wait(dve, s_mv, NT, run, NT)
                wait(dve, s_rstd, 1, run, 1)
                for t in range(NT):
                    dve.tensor_scalar(xn[:, t, :], X[:, slot, t, :], mv[:, t, 0:1], rstd[:, t:t + 1],
                                      ALU.subtract, ALU.mult).then_inc(s_xn, 1)

            F_LN = (stats_done, mv_done, rstd_done, xn_done)
            A_LN = (astats_done, amv_done, arstd_done, axn_done)

            def step(run, k, ins, before_max=False):
                ins.then_inc(route_step, 1)
                if before_max:
                    wait_by_memset(route_step, ROUTE_STEPS, run, k)
                else:
                    wait(dve, route_step, ROUTE_STEPS, run, k)

            def route_groups(run):
                wait(dve, gate_exp_done, 1, run, 1)
                step(run, 1, dve.tensor_scalar(r_den[:], r_exp[:], 1.0, None, ALU.add))
                step(run, 2, dve.reciprocal(r_score[:], r_den[:]))
                step(run, 3, dve.tensor_tensor(r_choice[:], r_score[:],
                                               gbias_sb[:].unsqueeze(1).to_broadcast([P, NT, E]), ALU.add))
                pairs = r_choice[:].rearrange("p t (g b a) -> p (t g) b a", g=GROUPS, a=2)
                step(run, 4, dve.tensor_tensor(r_max[:], pairs[:, :, :, 0], pairs[:, :, :, 1], ALU.max))
                step(run, 5, dve.tensor_tensor(r_min[:], pairs[:, :, :, 0], pairs[:, :, :, 1], ALU.min))
                step(run, 6, dve.tensor_tensor(r_top1[:], r_max[:, :, 0], r_max[:, :, 1], ALU.max))
                step(run, 7, dve.tensor_tensor(r_mid[:], r_max[:, :, 0], r_max[:, :, 1], ALU.min))
                step(run, 8, dve.tensor_tensor(r_low[:], r_min[:, :, 0], r_min[:, :, 1], ALU.max))
                step(run, 9, dve.tensor_tensor(r_top2[:], r_mid[:], r_low[:], ALU.max))
                step(run, 10, dve.tensor_tensor(r_group[:].rearrange("p t g -> p (t g)"), r_top1[:], r_top2[:],
                                                ALU.add))

            def route_mask(run):
                other = r_group[:].unsqueeze(2).to_broadcast([P, NT, GROUPS, GROUPS])
                own = r_group[:].unsqueeze(3).to_broadcast([P, NT, GROUPS, GROUPS])
                step(run, 11, dve.tensor_tensor(r_gt[:], other, own, ALU.is_gt))
                step(run, 12, dve.tensor_tensor(r_eq[:], other, own, ALU.is_equal))
                step(run, 13, dve.tensor_tensor(r_eq_tri[:], r_eq[:],
                                                tri[:].unsqueeze(1).to_broadcast([P, NT, GROUPS, GROUPS]), ALU.mult))
                step(run, 14, dve.tensor_tensor(r_before[:], r_gt[:], r_eq_tri[:], ALU.add))
                step(run, 15, dve.tensor_reduce(r_rank[:], r_before[:].rearrange("p t g j -> p (t g) j"), AX.X, ALU.add))
                step(run, 16, dve.tensor_scalar(r_gmask[:], r_rank[:], float(TOP_GROUPS), None, ALU.is_lt))
                step(run, 17, dve.tensor_tensor(r_masked[:].rearrange("p t (g i) -> p (t g) i", g=GROUPS),
                                                r_choice[:].rearrange("p t (g i) -> p (t g) i", g=GROUPS),
                                                r_gmask[:].unsqueeze(2).to_broadcast([P, NT * GROUPS, E // GROUPS]),
                                                ALU.mult), before_max=True)
                for t in range(NT):
                    ins = dve.max(r_top8[:, t, :], r_masked[:, t, :])
                step(run, 18, ins)

            def route_top(run):
                fourth = r_top8[:, :, TOP_K - 1:TOP_K].to_broadcast([P, NT, E])
                step(run, 19, dve.tensor_tensor(r_above[:], r_masked[:], fourth, ALU.is_gt))
                step(run, 20, dve.tensor_tensor(scan_a[:, :, 8:], r_masked[:], fourth, ALU.is_equal))
                step(run, 21, dve.tensor_copy(r_tie[:], scan_a[:, :, 8:]))
                src, dst = scan_a, scan_b
                for n, k in enumerate((1, 2, 4, 8)):
                    step(run, 22 + n, dve.tensor_tensor(dst[:, :, 8:], src[:, :, 8:], src[:, :, 8 - k:8 + E - k],
                                                        ALU.add))
                    src, dst = dst, src
                step(run, 26, dve.tensor_reduce(r_n_above[:], r_above[:], AX.X, ALU.add))
                step(run, 27, dve.tensor_scalar(r_room[:], r_n_above[:], -1.0, float(TOP_K), ALU.mult, ALU.add))

            def route_weights(run):
                step(run, 28, dve.tensor_tensor(r_fits[:], scan_a[:, :, 8:], r_room[:].unsqueeze(2)
                                                .to_broadcast([P, NT, E]), ALU.is_le))
                step(run, 29, dve.tensor_tensor(r_tie_in[:], r_fits[:], r_tie[:], ALU.mult))
                step(run, 30, dve.tensor_tensor(r_pick[:], r_tie_in[:], r_above[:], ALU.add))
                step(run, 31, dve.tensor_tensor(r_w[:], r_pick[:], r_masked[:], ALU.mult))
                step(run, 32, dve.tensor_reduce(r_sum[:], r_w[:], AX.X, ALU.add))
                step(run, 33, dve.tensor_scalar(r_sum_eps[:], r_sum[:], 1e-20, None, ALU.add))
                step(run, 34, dve.reciprocal(r_inv[:], r_sum_eps[:]))
                wait(dve, comb_psum, 1, run, 0)
                if isinstance(run, int) and run == 0:
                    dve.wait_ge(zeroed, 6)
                dve.scalar_tensor_tensor(r_comb[:], r_w[:], ROUTE_SCALE, r_inv[:].unsqueeze(2)
                                         .to_broadcast([P, NT, E]), ALU.mult, ALU.mult).then_inc(comb_done, 1)
                wait(dve, comb_done, 3, run, 1)
                dve.tensor_copy(comb[:, :, 0:E].bitcast(F32R), r_comb[:]).then_inc(comb_done, 1)
                wait(dve, comb_done, 3, run, 2)
                dve.tensor_tensor(comb[:, :, E:2 * E].bitcast(F32R), r_comb[:], comb[:, :, 0:E], ALU.subtract)\
                   .then_inc(comb_done, 1)

            def next_x_lo(run):
                wait(dve, xt_hi_done, 1, run, 1)
                dve.tensor_tensor(xt_next_lo[:], pA[:], xt_next_hi[:].bitcast(F32), ALU.subtract)\
                   .then_inc(xt_lo_done, 1)

            dve.wait_ge(x_in[0], 16)
            layernorm(0, F_LN, 0)
            dve.wait_ge(w_hi_done, 1)
            dve.tensor_tensor(gk_lo[:], gk_raw[:], gk_hi[:].bitcast(F32), ALU.subtract).then_inc(w_lo_done, 1)
            normalize(0, F_LN, 0)
            next_x_lo(0)
            dve.wait_ge(zeroed, 6)
            dve.wait_ge(const_in, 48)
            dve.wait_ge(route_in, 32)
            for n in range(WGP):
                cols = slice(n * WPC, (n + 1) * WPC)
                dve.wait_ge(w_hi_done, 2 + 2 * n)
                dve.tensor_tensor(wg_lo[:, cols], wg_raw[:, cols], wg_hi[:, cols].bitcast(F32), ALU.subtract)\
                   .then_inc(w_lo_done, 1)
                dve.wait_ge(w_hi_done, 3 + 2 * n)
                dve.tensor_tensor(wu_lo[:, cols], wu_raw[:, cols], wu_hi[:, cols].bitcast(F32), ALU.subtract)\
                   .then_inc(w_lo_done, 1)
                if n == 0:
                    route_groups(0)
                    route_mask(0)
                    route_top(0)
                    route_weights(0)

            def unit(u, attn, next_attn, last):
                a = u - LAG
                wait(dve, xt_lo_done, 1, u, 1)
                wait(dve, u_psum, CH, u, 0)
                dve.tensor_copy(xt_lo[:], xt_next_lo[:].bitcast(F32)).then_inc(xt_moved_lo, 1)
                if isinstance(u, int) and u == 1:
                    for c in range(4):
                        dve.wait_ge(attn_hi_done, c + 1)
                        dve.tensor_tensor(wq_lo[:, c, :].rearrange("p (j r d) -> p j r d", j=4, r=4),
                                          q_heads(wq_scaled, c),
                                          wq_hi[:, c, :].bitcast(F32).rearrange("p (j r d) -> p j r d", j=4, r=4),
                                          ALU.subtract).then_inc(attn_lo_done, 1)
                    dve.wait_ge(attn_hi_done, 6)
                    dve.tensor_tensor(wk_lo[:].rearrange("p (r d) -> p r d", d=HD),
                                      wk_raw[:].unsqueeze(1).to_broadcast([P, P // HD, HD]),
                                      wk_hi[:].bitcast(F32).rearrange("p (r d) -> p r d", d=HD), ALU.subtract)\
                       .then_inc(attn_lo_done, 1)
                    dve.tensor_tensor(wv_lo[:], wv_raw[:], wv_hi[:].bitcast(F32), ALU.subtract)\
                       .then_inc(attn_lo_done, 1)

                def q_part(c):
                    wait(dve, qk_hi_done, 5, a, c + 1)
                    dve.scalar_tensor_tensor(q_rep[:, c // 2, :, c % 2, :],
                                             qk_hi[:, c % 2, :].bitcast(F32).rearrange("p (i q) -> p i q", q=QB),
                                             beta[:, 0:1], q_banks[c][:].rearrange("p (i q) -> p i q", q=QB),
                                             ALU.mult, ALU.add).then_inc(qk_done, 1)

                def k_part():
                    wait(dve, qk_hi_done, 5, a, 5)
                    for j in range(4):
                        rows = slice(32 * j, 32 * j + 32)
                        dve.scalar_tensor_tensor(k_diag[rows, j, :], qk_hi[rows, 0, :].bitcast(F32), beta[rows, 1:2],
                                                 k_bank[rows, :], ALU.mult, ALU.add).then_inc(qk_done, 1)

                for t, e in schedule(attn):
                    if attn and t == 0:
                        if isinstance(u, int):
                            dve.wait_ge(zeroed, 8)
                        q_part(0)
                        q_part(1)
                    if e is not None:
                        wait(dve, tanh_done, CH, u, e + 1)
                        dve.scalar_tensor_tensor(sg[:], th[:], 1.0, pG[:], ALU.add, ALU.mult).then_inc(sg_done, 1)
                        wait(dve, sg_done, CH, u, e + 1)
                        wait(dve, u_psum, CH, u, e + 1)
                        if e == CH - 1:
                            wait(dve, down_done, CH, u, e - 1)
                            dve.scalar_tensor_tensor(hid[:, e % 2, :], sg[:], 0.5, pU[:], ALU.mult, ALU.mult)\
                               .then_inc(hid_done, 1)
                        else:
                            dve.scalar_tensor_tensor(gu[:], sg[:], 0.5, pU[:], ALU.mult, ALU.mult)\
                               .then_inc(gu_done, 1)
                    if attn and t == 0:
                        q_part(2)
                        q_part(3)
                        k_part()
                    if e == 2 and not last:
                        next_x_lo(u + 1)
                    if e == 5 and next_attn:
                        wait(dve, xa_hi_done, 1, u - 1, 1)
                        dve.tensor_tensor(xa_lo[:], pA[:], xa_hi[:].bitcast(F32), ALU.subtract)\
                           .then_inc(xa_lo_done, 1)
                    if e is not None and e < CH - 1:
                        wait(dve, gu_done, NP2, u, e + 1)
                        wait(dve, c_psum, NP2, u, e + 1)
                        if e == 0:
                            wait(dve, down_done, CH, u, 0)
                        elif e >= 2:
                            wait(dve, down_done, CH, u, e - 1)
                        dve.tensor_tensor(hid[:, e % 2, :], gu[:], pA[:], ALU.mult).then_inc(hid_done, 1)
                    if e == 1 and not (isinstance(u, int) and u == 0):
                        wait(dve, y_back, 1, u, 0)
                        dve.scalar_tensor_tensor(X[:, u - 1].rearrange("p t d -> p (t d)"), pY[:], 0.5,
                                                 X[:, u - 1].rearrange("p t d -> p (t d)"), ALU.mult, ALU.add)\
                           .then_inc(x_added, 1)
                    if attn and 1 <= t < NBLK + 1:
                        i = t - 1
                        wait(dve, s_psum, NBLK, a, i + 1)
                        wait(dve, exp_done, NBLK, a, i)
                        dve.tensor_reduce(neg_max[:, 0:4], pS0[:].rearrange("p (s k) -> p s k", s=4), AX.X, ALU.max,
                                          negate=True)
                        dve.tensor_reduce(neg_max[:, 4:8], pS1[:].rearrange("p (s k) -> p s k", s=4), AX.X, ALU.max,
                                          negate=True).then_inc(max_done, 1)
                    if attn and 2 <= t < NBLK + 2:
                        i = t - 2
                        o_all = pO[:, 0:8 * (HD + 1)].rearrange("p (s d) -> p s d", d=HD + 1)
                        wait(dve, o_psum, NBLK, a, i + 1)
                        dve.reciprocal(o_inv[:], o_all[:, :, HD]).then_inc(o_inv_done, 1)
                        wait(dve, o_inv_done, NBLK, a, i + 1)
                        wait(dve, ot_psum, NBLK, a, i)
                        dve.tensor_tensor(o_norm[:], o_all[:, :, 0:HD], o_inv[:].unsqueeze(2)
                                          .to_broadcast([P, 8, HD]), ALU.mult).then_inc(o_norm_done, 1)
                    if e == 0 and not last:
                        if isinstance(u, int) and u + 1 < NB:
                            dve.wait_ge(x_in[u + 1], 16)
                        else:
                            wait_apart(dve, attn_added, 1, u, 2 - NB)
                        layernorm(u + 1, F_LN, u + 1)
                    if e == 1 and not last:
                        normalize(u + 1, F_LN, u + 1)
                    if e == 3 and next_attn:
                        wait_apart(dve, x_added, 1, u, 0)
                        layernorm(u - 1, A_LN, u - 1)
                    if e == 4 and next_attn:
                        normalize(u - 1, A_LN, u - 1)
                    if not last:
                        if e == 4:
                            route_groups(u + 1)
                        if e == 5:
                            route_mask(u + 1)
                        if e == 6:
                            route_top(u + 1)
                        if e == 7:
                            route_weights(u + 1)
                if attn:
                    wait(dve, attn_psum, 1, a, 1)
                    dve.tensor_tensor(X[:, u - LAG + NB].rearrange("p t d -> p (t d)"), pS0[:],
                                      X[:, u - LAG].rearrange("p t d -> p (t d)"), ALU.add).then_inc(attn_added, 1)

            units(dve, unit)
            dve.wait_ge(y_back, UNITS)
            dve.scalar_tensor_tensor(X[:, UNITS - 1].rearrange("p t d -> p (t d)"), pY[:], 0.5,
                                     X[:, UNITS - 1].rearrange("p t d -> p (t d)"), ALU.mult, ALU.add)\
               .then_inc(x_added, 1)

        @block.tensor
        def _(pe):
            def three(dst, w_hi, w_lo, x_hi, x_lo, start=True):
                pe.matmul(dst, w_hi, x_hi, start=start, stop=False)
                pe.matmul(dst, w_lo, x_hi, start=False, stop=False)
                return pe.matmul(dst, w_hi, x_lo, start=False, stop=True)

            def to_columns(src, done, xn_sem, run, hid_wait):
                hid_wait()
                wait(pe, xn_sem, NT, run, NT)
                for t in range(NT):
                    ins = pe.transpose(pA[:, P * t:P * (t + 1)], src[:, t, :], ident[:])
                ins.then_inc(done, 1)

            def logits(run):
                wait(pe, xt_hi_done, 1, run, 1)
                wait(pe, xt_lo_done, 1, run, 1)
                for t in range(NT):
                    tok = slice(P * t, P * (t + 1))
                    dst = pA[:, E * t:E * (t + 1)]
                    pe.matmul(dst, xt_next_hi[:, tok], gk_hi[:], start=True, stop=False)
                    pe.matmul(dst, xt_next_hi[:, tok], gk_lo[:], start=False, stop=False)
                    pe.matmul(dst, xt_next_lo[:, tok], gk_hi[:], start=False, stop=False)
                    ins = pe.matmul(dst, xt_next_lo[:, tok], gk_lo[:], start=False, stop=True)
                ins.then_inc(logits_psum, 1)

            pe.wait_ge(const_in, 48)
            to_columns(xn, xt_psum, xn_done, 0, lambda: None)
            pe.wait_ge(w_hi_done, 1)
            pe.wait_ge(w_lo_done, 1)
            logits(0)

            def unit(u, attn, next_attn, last):
                a = u - LAG
                first = isinstance(u, int) and u == 0

                def down(n, e):
                    wait(pe, hid_done, CH, n, e + 1)
                    if e == 0:
                        wait(pe, x_added, 1, n, 0)
                    if isinstance(n, int) and n == 0 and e == 0:
                        pe.wait_ge(wd_in, 16)
                    pe.matmul(pY[:], wd_sb[:, e, :], hid[:, e % 2, :], start=(e == 0), stop=(e == CH - 1))\
                      .then_inc(down_done, 1)

                def transpose_probs(i, h):
                    wait(pe, exp_done, NBLK, a, i + 1)
                    wait(pe, t_copied, 2 * NBLK, a, 2 * i + h)
                    if i == 0 and h == 0:
                        wait(pe, v_done, 1, a, 1)
                    for s in range(4):
                        ins = pe.transpose(pT[:, P * s:P * (s + 1)], prob[:, 4 * h + s, :], ident[:])
                    ins.then_inc(t_psum, 1)

                def weighted_values(i, h):
                    wait(pe, t_copied, 2 * NBLK, a, 2 * i + h + 1)
                    wait(pe, ot_copied, NBLK, a, i)
                    wait(pe, o_norm_done, NBLK, a, i)
                    for s in range(4 * h, 4 * h + 4):
                        ins = pe.matmul(pO[:, (HD + 1) * s:(HD + 1) * (s + 1)], prob_t[:, s, :], v_one[:, i, :],
                                        start=True, stop=True)
                    if h == 1:
                        ins.then_inc(o_psum, 1)

                def turn_output(i):
                    wait_apart(pe, o_norm_done, NBLK, a, i + 1)
                    pe.transpose(pO[0:P // 2, O_T:O_T + P], o_norm[:].rearrange("p s d -> p (s d)"), ident[:])\
                      .then_inc(ot_psum, 1)

                def scores(i):
                    wait(pe, exp_done, NBLK, a, i)
                    if i == 0:
                        wait(pe, qk_done, 8, a, 8)
                    ks = key_start(i)
                    for h, bank in enumerate((pS0, pS1)):
                        pe.matmul(bank[:], ident_bf[:], mask[:, mask_kind(i):mask_kind(i) + 1, :]
                                  .to_broadcast([P, 4, P]), start=True, stop=False)
                        ins = pe.matmul(bank[:], q_rep[:, h, i, :, :].rearrange("p c q -> p (c q)"),
                                        k_diag[:, :, ks:ks + P], start=False, stop=True)
                    ins.then_inc(s_psum, 1)

                wait(pe, hid_done, CH, u, 0)
                wait(pe, comb_done, 3, u, 3)
                if first:
                    pe.wait_ge(gate_exp_done, 1)
                for t in range(NT):
                    ins = pe.transpose(pA[:, P * t:P * (t + 1)], comb[:, t, :], ident[:])
                ins.then_inc(comb_psum, 1)

                for t, e in schedule(attn):
                    if attn and t == 0:
                        if isinstance(u, int):
                            pe.wait_ge(attn_lo_done, 6)
                            pe.wait_ge(zeroed, 8)
                            pe.wait_ge(consts_ready, 3)
                        wait(pe, xa_hi_done, 1, a, 1)
                        wait(pe, xa_lo_done, 1, a, 1)
                        wait(pe, exp_done, NBLK, a, 0)
                        wait(pe, t_copied, 2 * NBLK, a, 0)
                        wait(pe, ot_copied, NBLK, a, 0)
                        for c in range(3):
                            three(q_banks[c][:], wq_hi[:, c, :], wq_lo[:, c, :], xa_hi[:], xa_lo[:])\
                                .then_inc(qk_psum, 1)
                    if attn and 3 <= t < NBLK + 3:
                        turn_output(t - 3)
                    if attn and 2 <= t < NBLK + 2:
                        transpose_probs(t - 2, 0)
                    if e is not None:
                        if e == 0:
                            wait(pe, xt_moved_hi, 1, u, 1)
                            wait(pe, xt_moved_lo, 1, u, 1)
                        if first:
                            n = (P * (e + 1) - 1) // WPC
                            pe.wait_ge(w_lo_done, 3 + 2 * n)
                        wait(pe, sg_done, CH, u, e)
                        cols = slice(P * e, P * (e + 1))
                        three(pG[:], wg_hi[:, cols], wg_lo[:, cols], xt_hi[:], xt_lo[:]).then_inc(g_psum, 1)
                        wait(pe, gu_done, NP2, u, min(e, NP2))
                        if e == 0:
                            wait(pe, hid_done, CH, u, 0)
                        three(pU[:], wu_hi[:, cols], wu_lo[:, cols], xt_hi[:], xt_lo[:]).then_inc(u_psum, 1)
                    if attn and t == 0:
                        wait(pe, attn_added, 1, a, 0)
                        three(q_banks[3][:], wq_hi[:, 3, :], wq_lo[:, 3, :], xa_hi[:], xa_lo[:])\
                            .then_inc(qk_psum, 1)
                        wait(pe, qk_done, 8, a, 1)
                        three(k_bank[:], wk_hi[:], wk_lo[:], xa_hi[:], xa_lo[:]).then_inc(qk_psum, 1)
                        wait(pe, qk_done, 8, a, 2)
                        for i in range(NBLK):
                            keys = slice(key_start(i), key_start(i) + P)
                            ins = three(v_bank[:, HD * i:HD * (i + 1)], xa_hi[:, keys], xa_lo[:, keys],
                                        wv_hi[:], wv_lo[:])
                        ins.then_inc(v_psum, 1)
                    if attn and 2 <= t < NBLK + 2:
                        transpose_probs(t - 2, 1)
                    if e == 0 and not first:
                        down(u - 1, CH - 1)
                    if e == 2 and not last:
                        to_columns(xn, xt_psum, xn_done, u + 1, lambda: wait(pe, hid_done, CH, u, e))
                    if e == 3 and not last:
                        wait(pe, hid_done, CH, u, e)
                        logits(u + 1)
                    if e == 5 and next_attn:
                        to_columns(xn, xa_psum, axn_done, u - 1, lambda: wait(pe, hid_done, CH, u, e))
                    if e == 1 and not first:
                        wait(pe, y_copied, 1, u, 0)
                        for s in range(NT):
                            ins = pe.transpose(pY[:, P * s:P * (s + 1)], y_sb[:, P * s:P * (s + 1)], ident[:])
                        ins.then_inc(y_back, 1)
                    if e is not None and e < NP2:
                        wait(pe, hid_done, CH, u, e)
                        if e == 0:
                            wait(pe, comb_t_done, 1, u, 1)
                            if first:
                                pe.wait_ge(consts_ready, 1)
                        if e == 2 and not last:
                            wait(pe, xt_lo_done, 1, u + 1, 1)
                        if e == 3 and not last:
                            wait(pe, gate_exp_done, 1, u + 1, 1)
                        if e == 5 and next_attn:
                            wait(pe, xa_lo_done, 1, u - 1, 1)
                        pe.matmul(pA[:], sel[:, e, :], comb_t[:], start=True, stop=True).then_inc(c_psum, 1)
                    if attn and 2 <= t < NBLK + 2:
                        weighted_values(t - 2, 0)
                    if attn and 1 <= t < NBLK + 1:
                        scores(t - 1)
                    if attn and 2 <= t < NBLK + 2:
                        weighted_values(t - 2, 1)
                    if attn and t == TICKS - 1:
                        wait(pe, ot_copied, NBLK, a, NBLK)
                        for s in range(NT):
                            tok = slice(P * s, P * (s + 1))
                            dst = pS0[:, P * s:P * (s + 1)]
                            pe.matmul(dst, o_t[:, 0, tok], wf_sb[:, 0, :], start=True, stop=False)
                            pe.matmul(dst, o_t[:, 1, tok], wf_sb[:, 1, :], start=False, stop=False)
                            ins = pe.matmul(dst, ones_row[:], bf_sb[:], start=False, stop=True)
                        ins.then_inc(attn_psum, 1)
                    if e is not None and e >= 1:
                        down(u, e - 1)

            units(pe, unit)
            pe.wait_ge(hid_done, CH * UNITS)
            pe.matmul(pY[:], wd_sb[:, CH - 1, :], hid[:, (CH - 1) % 2, :], start=False, stop=True)\
              .then_inc(down_done, 1)
            pe.wait_ge(y_copied, UNITS)
            for s in range(NT):
                ins = pe.transpose(pY[:, P * s:P * (s + 1)], y_sb[:, P * s:P * (s + 1)], ident[:])
            ins.then_inc(y_back, 1)


def kernel(**inputs):
    import numpy as np
    import concourse.bacc as bacc
    from concourse.bass_utils import run_bass_kernel_spmd

    def a(name):
        return np.asarray(inputs[name])

    def put(z):
        return np.ascontiguousarray(z)

    wg = np.concatenate([a("L0_ffn_w_gate").transpose(1, 0, 2).reshape(D, E * M), a("L0_ffn_sw_gate")], 1)
    wu = np.concatenate([a("L0_ffn_w_up").transpose(1, 0, 2).reshape(D, E * M), a("L0_ffn_sw_up")], 1)
    wd = np.concatenate([a("L0_ffn_w_down").reshape(NP2, P, D), a("L0_ffn_sw_down")[None]], 0).transpose(1, 0, 2)
    q = np.arange(P)[:, None] % QB
    k = np.arange(P)[None, :]
    first_key = [0, -WINDOW, -QB]
    mask = np.stack([np.where(np.abs(q - (k + s)) <= WINDOW, 0.0, -1e30) for s in first_key], 1).astype(np.float32)
    sel = np.zeros((P, NP2, P), np.float32)
    for e in range(E):
        sel[[e, E + e], e // 2, (e % 2) * M:(e % 2 + 1) * M] = 1.0
    tri = np.broadcast_to(np.tril(np.ones((GROUPS, GROUPS), np.float32), -1), (P, GROUPS, GROUPS))
    part = np.arange(P) // HD % 4
    beta = np.stack([np.where(part >= 2, -1.0, 0.0), np.where(part % 2 == 1, -1.0, 0.0)], 1).astype(np.float32)
    arrays = {
        "x": put(a("L0_attn_x").reshape(NB * SEQ, D)), "wg": put(wg), "wu": put(wu), "wd": put(wd),
        "gk": put(a("L0_ffn_gate_kernel")), "gbias": put(np.broadcast_to(a("L0_ffn_gate_bias"), (P, E))),
        "wq": put(a("L0_attn_Wq").T), "wk": put(a("L0_attn_Wk").T), "wv": put(a("L0_attn_Wv").T),
        "wf": put(a("L0_attn_Wf").T.reshape(2, P // 2, D).transpose(1, 0, 2)),
        "bf": put(a("L0_attn_bf").reshape(1, D)),
        "ident_in": np.eye(P, dtype=np.float32), "mask_in": put(mask), "sel_in": sel, "tri_in": put(tri),
        "beta_in": put(beta),
    }
    nc = bacc.Bacc("TRN2", target_bir_lowering=False, num_devices=1)
    args = [nc.dram_tensor(n, z.shape, mybir.dt.from_np(z.dtype), kind="ExternalInput").ap()
            for n, z in arrays.items()]
    out = nc.dram_tensor("out", (NB * SEQ, D), F32, kind="ExternalOutput").ap()
    macaron(nc, *args, out)
    r = run_bass_kernel_spmd(nc, [arrays], core_ids=[0])
    return r.results[0]["out"].reshape(NB, SEQ, D)
```

```python
from contextlib import ExitStack

import concourse.bass as bass
from concourse import mybir

ALU = mybir.AluOpType
ACT = mybir.ActivationFunctionType
AX = mybir.AxisListType
F32 = mybir.dt.float32
F32R = mybir.dt.float32r
BF16 = mybir.dt.bfloat16

P = 128
NB, SEQ, D = 4, 512, 128
NT = SEQ // P
E, M = 16, 64
CH = E * M // P + 1
NP2 = CH - 1
GROUPS, TOP_GROUPS, TOP_K, ROUTE_SCALE = 4, 2, 4, 2.5
HD, WINDOW = 8, 32
QB = 64
NBLK = SEQ // QB
EPS = 1e-5
UNITS = 2 * NB
LAG = 2

TICKS = NBLK + 3
CHUNK_TICKS = [0, 1, 2, 3, 5, 6, 7, 9, 10]
X_COLUMNS = {True: 4, False: 2}
LOGITS = {True: 4, False: 3}
XA_COLUMNS = {True: 8, False: 5}
Y_DONE = {True: 1, False: 0}
Y_ROWS = {True: 2, False: 1}
X_NORM = {True: 1, False: 0}
XA_NORM = {True: 6, False: 3}
HIDS = 3
ROUTE_STEPS = 27
ROUTE_ATTN = {5: (1, 2, 2), 6: (1, 2, 2), 7: (1, 2, 2), 8: (2, 2, 2), 9: (1, 1, 1), 10: (1, 1, 1)}
ROUTE_ALONE = {4: (1, 2, 2), 5: (1, 2, 2), 6: (2, 2, 2), 7: (1, 2, 2), 8: (2, 2, 2)}
ALONE = {0: 0, 1: 1, UNITS - 2: 2, UNITS - 1: 3}


def key_start(i):
    return min(max(QB * i - WINDOW, 0), SEQ - P)


def mask_kind(i):
    return 0 if i == 0 else 2 if i == NBLK - 1 else 1


def macaron(nc, x, wg, wu, wd, gk, gbias, wq, wk, wv, wf, ident_in, mask_in, sel_in, tri_in, beta_in, out):
    ctx = ExitStack()
    with ctx:
        def sb(name, shape, dt=F32):
            return ctx.enter_context(nc.sbuf_tensor(name, shape, dt))

        def ps(name, shape):
            return ctx.enter_context(nc.psum_tensor(name, shape, F32))

        def sem(name):
            return ctx.enter_context(nc.semaphore(name))

        X = sb("X", [P, UNITS, NT, D])
        wg_raw = sb("wg_raw", [P, CH * P])
        wu_raw = sb("wu_raw", [P, CH * P])
        wg_hi, wg_lo = sb("wg_hi", [P, CH * P], F32R), sb("wg_lo", [P, CH * P], F32R)
        wu_hi, wu_lo = sb("wu_hi", [P, CH * P], F32R), sb("wu_lo", [P, CH * P], F32R)
        wd_sb = sb("wd_sb", [P, CH, D])
        gk_raw = sb("gk_raw", [P, E])
        gk_parts = sb("gk_parts", [P, 2, E], F32R)
        gbias_sb = sb("gbias_sb", [P, E])
        wq_raw = sb("wq_raw", [P, D])
        wq_scaled = sb("wq_scaled", [P, D])
        wk_raw = sb("wk_raw", [P, HD])
        wv_raw = sb("wv_raw", [P, HD])
        wq_hi, wq_lo = sb("wq_hi", [P, 4, P], F32R), sb("wq_lo", [P, 4, P], F32R)
        wk_hi, wk_lo = sb("wk_hi", [P, P], F32R), sb("wk_lo", [P, P], F32R)
        wv_parts = sb("wv_parts", [P, 2, HD], F32R)
        v_lo = sb("v_lo", [P, NBLK, HD])
        wf_sb = sb("wf_sb", [P // 2 + 1, 2, D])
        ident = sb("ident", [P, P])
        ident_bf = sb("ident_bf", [P, P], BF16)
        mask_raw = sb("mask_raw", [P, 3, P])
        mask = sb("mask", [P, 3, P], BF16)
        sel_raw = sb("sel_raw", [P, NP2, P])
        sel = sb("sel", [P, NP2, P], F32R)
        tri = sb("tri", [P, GROUPS, GROUPS])
        beta = sb("beta", [P, 2])
        half = sb("half", [P, NT])
        eps = sb("eps", [P, NT])
        pause = sb("pause", [P, 1])

        stats = sb("stats", [P, NT, 6])
        mv = sb("mv", [P, NT, 2])
        amv = sb("amv", [P, NT, 2])
        var_eps = sb("var_eps", [P, NT])
        rstd = sb("rstd", [P, NT])
        x_centred = sb("x_centred", [P, NT, D])
        xn = sb("xn", [P, NT, D])
        xt_next_hi, xt_next_lo = sb("xt_next_hi", [P, SEQ], F32R), sb("xt_next_lo", [P, SEQ], F32R)
        xt_hi, xt_lo = sb("xt_hi", [P, SEQ], F32R), sb("xt_lo", [P, SEQ], F32R)
        xa_hi, xa_lo = sb("xa_hi", [P, SEQ], F32R), sb("xa_lo", [P, SEQ], F32R)
        r_exp = sb("r_exp", [P, NT, E])
        r_logit_lo = sb("r_logit_lo", [P, NT, E])
        r_logit = sb("r_logit", [P, NT, E])
        r_den = sb("r_den", [P, NT, E])
        r_score = sb("r_score", [P, NT, E])
        r_choice = sb("r_choice", [P, NT, E])
        r_pair = sb("r_pair", [P, NT * GROUPS, 6])
        r_group = sb("r_group", [P, NT, GROUPS])
        r_gt = sb("r_gt", [P, NT, GROUPS, GROUPS])
        r_eq = sb("r_eq", [P, NT, GROUPS, GROUPS])
        r_eq_tri = sb("r_eq_tri", [P, NT, GROUPS, GROUPS])
        r_before = sb("r_before", [P, NT, GROUPS, GROUPS])
        r_rank = sb("r_rank", [P, NT * GROUPS])
        r_masked = sb("r_masked", [P, NT, E])
        r_top8 = sb("r_top8", [P, NT, 8])
        r_above = sb("r_above", [P, NT, E])
        r_tie = sb("r_tie", [P, NT, 1 + E])
        r_carry = sb("r_carry", [P, NT, 1 + E])
        r_count = sb("r_count", [P, NT, 1 + E])
        r_tie_in = sb("r_tie_in", [P, NT, E])
        r_pick = sb("r_pick", [P, NT, E])
        r_w = sb("r_w", [P, NT, E])
        r_sum = sb("r_sum", [P, NT])
        r_sum_eps = sb("r_sum_eps", [P, NT])
        r_inv = sb("r_inv", [P, NT])
        r_comb = sb("r_comb", [P, NT, E])
        comb = sb("comb", [P, NT, P])
        comb_t = sb("comb_t", [P, SEQ], F32R)

        th = sb("th", [P, 2, SEQ])
        sg = sb("sg", [P, 2, SEQ])
        gu = sb("gu", [P, 2, SEQ])
        c_sb = sb("c_sb", [P, 2, SEQ])
        hid = sb("hid", [P, HIDS, SEQ])
        y_sb = sb("y_sb", [P, SEQ])

        qk_hi = sb("qk_hi", [P, 2, SEQ], F32R)
        q_rep = sb("q_rep", [P, 2, NBLK, 2, QB], F32R)
        k_diag = sb("k_diag", [P, 4, SEQ], F32R)
        v_one = sb("v_one", [P, NBLK, 32])
        neg_max = sb("neg_max", [P, 8])
        prob = sb("prob", [P, 2, 8, P])
        prob_t = sb("prob_t", [P, 2, 8, P])
        o_inv = sb("o_inv", [P, 8])
        o_norm = sb("o_norm", [P, 8, HD])
        o_raw = sb("o_raw", [P, 2 * P])
        o_t = sb("o_t", [P // 2 + 1, 2, SEQ])

        pG, pU, pA, pY = ps("pG", [P, SEQ]), ps("pU", [P, SEQ]), ps("pA", [P, SEQ]), ps("pY", [P, SEQ])
        pS0, pS1, pT, pO = ps("pS0", [P, SEQ]), ps("pS1", [P, SEQ]), ps("pT", [P, SEQ]), ps("pO", [P, SEQ])
        BACK = 2 * P
        q_banks = [pS1, pT, pO, pS0]
        k_bank, v_bank = pS1, pT

        x_in = [sem(f"x_in{b}") for b in range(NB)]
        ident_loaded, const_in, wg_in, wu_in, wd_in, attn_w_in, route_in, out_done = (
            sem(n) for n in ("ident_loaded", "const_in", "wg_in", "wu_in", "wd_in", "attn_w_in", "route_in", "out_done"))
        zeroed, consts_ready = sem("zeroed"), sem("consts_ready")
        w_hi_done, w_lo_done = sem("w_hi_done"), sem("w_lo_done")
        wq_scaled_done, attn_hi_done, attn_lo_done = sem("wq_scaled_done"), sem("attn_hi_done"), sem("attn_lo_done")
        stats_done, mv_done, eps_done, rstd_done, centred_done, xn_done = (
            sem(n) for n in ("stats_done", "mv_done", "eps_done", "rstd_done", "centred_done", "xn_done"))
        astats_done, amv_done, aeps_done, arstd_done, acentred_done, axn_done = (
            sem(n) for n in ("astats_done", "amv_done", "aeps_done", "arstd_done", "acentred_done", "axn_done"))
        xt_psum, xt_hi_done, xt_lo_done = sem("xt_psum"), sem("xt_hi_done"), sem("xt_lo_done")
        xa_psum, xa_hi_done, xa_lo_done = sem("xa_psum"), sem("xa_hi_done"), sem("xa_lo_done")
        logits_psum, logits_lo_done, logits_done = sem("logits_psum"), sem("logits_lo_done"), sem("logits_done")
        gate_exp_done, route_step = sem("gate_exp_done"), sem("route_step")
        comb_psum, comb_t_done = sem("comb_psum"), sem("comb_t_done")
        xt_moved_hi, xt_moved_lo = sem("xt_moved_hi"), sem("xt_moved_lo")
        g_psum, u_psum, c_psum = sem("g_psum"), sem("u_psum"), sem("c_psum")
        tanh_done, sg_done, gu_done, hid_done, down_done = (
            sem(n) for n in ("tanh_done", "sg_done", "gu_done", "hid_done", "down_done"))
        c_copied = sem("c_copied")
        y_copied, y_back, x_added = sem("y_copied"), sem("y_back"), sem("x_added")
        qk_psum, qk_hi_done, qk_done, v_psum, v_lo_done, v_done = (
            sem(n) for n in ("qk_psum", "qk_hi_done", "qk_done", "v_psum", "v_lo_done", "v_done"))
        s_psum, max_done, exp_done, t_psum, t_copied = (
            sem(n) for n in ("s_psum", "max_done", "exp_done", "t_psum", "t_copied"))
        o_psum, o_copied, back_psum, o_inv_done, o_norm_done, ot_psum, ot_copied = (
            sem(n) for n in ("o_psum", "o_copied", "back_psum", "o_inv_done", "o_norm_done", "ot_psum", "ot_copied"))
        attn_psum, attn_added = sem("attn_psum"), sem("attn_added")

        WGP = 3
        WPC = CH * P // WGP

        def g_bank(attn, e):
            return pS0 if not attn and e % 2 else pG

        def u_bank(attn, e):
            return pS1 if not attn and e % 2 else pU

        def c_bank(attn, e):
            return pT if not attn and e % 2 else pA

        def prep_bank(attn):
            return pA if attn else pO

        def wait(eng, s, per, index, k):
            n = index * per + k
            if not isinstance(n, int) or n > 0:
                eng.wait_ge(s, n)

        def wait_apart(eng, s, per, index, k):
            if isinstance(index, int):
                wait(eng, s, per, index, k)
            else:
                n = eng.snap(index * per + k)
                eng.wait_ge(zeroed, 9)
                eng.wait_ge(s, n)

        def schedule(attn):
            if attn:
                return [(t, CHUNK_TICKS.index(t) if t in CHUNK_TICKS else None) for t in range(TICKS)]
            return [(t, t) for t in range(CH)]

        def later_attention(u):
            return not isinstance(u, int) or LAG < u <= LAG + NB

        def q_heads(w, c):
            h0 = 8 * (c % 2) + 4 * (c // 2)
            return w[:, HD * h0:HD * (h0 + 4)].rearrange("p (j d) -> p j d", d=HD).unsqueeze(2)\
                .to_broadcast([P, 4, 4, HD])

        def units(eng, unit):
            unit(0, False, False, False)
            unit(1, False, True, False)
            unit(2, True, True, False)
            with eng.Fori(3, 5) as u:
                unit(u, True, True, False)
            unit(5, True, False, False)
            unit(6, False, False, False)
            unit(7, False, False, True)

        block = ctx.enter_context(nc.Block())

        @block.sync
        def _(sp):
            x_t = x.rearrange("(u t p) d -> u p t d", p=P, t=NT)
            out_t = out.rearrange("(u t p) d -> u p t d", p=P, t=NT)
            sp.dma_start(X[:, 0], x_t[0]).then_inc(x_in[0], 16)
            sp.dma_start(ident[:], ident_in).then_inc(ident_loaded, 16)
            sp.dma_start(tri[:], tri_in).then_inc(const_in, 16)
            sp.dma_start(gk_raw[:], gk).then_inc(route_in, 16)
            sp.dma_start(gbias_sb[:], gbias).then_inc(route_in, 16)
            sp.dma_start(wg_raw[:], wg).then_inc(wg_in, 16)
            sp.dma_start(wu_raw[:], wu).then_inc(wu_in, 16)
            sp.dma_start(sel_raw[:], sel_in).then_inc(const_in, 16)
            sp.dma_start(wd_sb[:], wd).then_inc(wd_in, 16)
            for b in range(1, NB):
                sp.dma_start(X[:, b], x_t[b]).then_inc(x_in[b], 16)
            sp.dma_start(mask_raw[:], mask_in).then_inc(attn_w_in, 16)
            sp.dma_start(beta[:], beta_in).then_inc(attn_w_in, 16)
            sp.dma_start(wq_raw[:], wq).then_inc(attn_w_in, 16)
            sp.dma_start(wk_raw[:], wk).then_inc(attn_w_in, 16)
            sp.dma_start(wv_raw[:], wv).then_inc(attn_w_in, 16)
            sp.dma_start(wf_sb[:], wf).then_inc(attn_w_in, 16)
            for u in range(NB, UNITS):
                sp.wait_ge(x_added, u + 1)
                sp.dma_start(out_t[u - NB], X[:, u]).then_inc(out_done, 16)
            sp.wait_ge(out_done, 16 * NB)

        @block.gpsimd
        def _(pool):
            pool.memset(half[:], -0.5).then_inc(zeroed, 1)
            pool.memset(eps[:], EPS).then_inc(zeroed, 1)
            pool.memset(r_carry[:], 1.0).then_inc(zeroed, 1)
            pool.memset(comb[:], 0.0).then_inc(zeroed, 1)
            pool.wait_ge(zeroed, 4)
            pool.memset(r_carry[:, :, 0:1], 0.0).then_inc(zeroed, 1)

            def rstd_of(mv, mv_sem, eps_sem, rstd_sem, run):
                wait(pool, mv_sem, NT, run, NT)
                pool.tensor_tensor(var_eps[:], mv[:, :, 1], eps[:], ALU.add).then_inc(eps_sem, 1)
                wait(pool, eps_sem, 1, run, 1)
                pool.tensor_tensor(rstd[:], var_eps[:], half[:], ALU.pow).then_inc(rstd_sem, 1)

            pool.wait_ge(zeroed, 2)
            rstd_of(mv, mv_done, eps_done, rstd_done, 0)
            pool.memset(v_one[:], 0.0).then_inc(zeroed, 1)
            pool.memset(k_diag[:].bitcast(F32), 0.0).then_inc(zeroed, 1)
            pool.wait_ge(zeroed, 7)
            pool.memset(o_t[P // 2:P // 2 + 1, :, :], 1.0).then_inc(zeroed, 1)
            pool.wait_ge(zeroed, 8)
            pool.memset(v_one[:, :, HD:HD + 1], 1.0).then_inc(zeroed, 1)

            def normalize(slot, mv, centred_sem, xn_sem, rstd_sem, run, first_run):
                wait(pool, rstd_sem, 1, run, 1)
                pool.tensor_tensor(x_centred[:], X[:, slot], mv[:, :, 0:1].to_broadcast([P, NT, D]), ALU.subtract)\
                    .then_inc(centred_sem, 1)
                wait(pool, centred_sem, 1, run, 1 - first_run)
                pool.tensor_tensor(xn[:], x_centred[:], rstd[:].unsqueeze(2).to_broadcast([P, NT, D]), ALU.mult)\
                    .then_inc(xn_sem, 1)

            def unit(u, attn, next_attn, last):
                for t, e in schedule(attn):
                    if t == X_NORM[attn] and not last:
                        rstd_of(mv, mv_done, eps_done, rstd_done, u + 1)
                        normalize(u + 1, mv, centred_done, xn_done, rstd_done, u + 1, 1)
                    if not attn and e < NP2:
                        wait(pool, gu_done, NP2, u, e + 1)
                        wait(pool, c_copied, NP2, ALONE[u], e + 1)
                        wait(pool, down_done, CH, u, e - HIDS + 1)
                        pool.tensor_tensor(hid[:, e % HIDS, :], gu[:, e % 2, :], c_sb[:, e % 2, :], ALU.mult)\
                            .then_inc(hid_done, 1)
                    if t == XA_NORM[attn] and next_attn:
                        rstd_of(amv, amv_done, aeps_done, arstd_done, u - 1)
                        normalize(u - 1, amv, acentred_done, axn_done, arstd_done, u - 1, 0)

            units(pool, unit)

        @block.scalar
        def _(act):
            def next_x(run, bank):
                wait(act, xt_psum, 1, run, 1)
                act.activation(xt_next_hi[:], bank[:], ACT.Copy).then_inc(xt_hi_done, 1)

            def logits_lo(run, bank):
                wait(act, logits_psum, 1, run, 1)
                act.activation(r_logit_lo[:], bank[:, 0:NT * 2 * E].rearrange("p (t h e) -> p t h e", t=NT, h=2)
                               [:, :, 1, :], ACT.Copy).then_inc(logits_lo_done, 1)

            def gate_exp(run):
                wait(act, logits_done, 1, run, 1)
                act.activation(r_exp[:], r_logit[:], ACT.Exp, scale=-1.0).then_inc(gate_exp_done, 1)

            act.wait_ge(route_in, 32)
            act.activation(gk_parts[:, 0], gk_raw[:], ACT.Copy).then_inc(w_hi_done, 1)
            next_x(0, pO)

            def weights_hi(n):
                cols = slice(n * WPC, (n + 1) * WPC)
                act.wait_ge(wg_in, 16)
                act.activation(wg_hi[:, cols], wg_raw[:, cols], ACT.Copy).then_inc(w_hi_done, 1)
                act.wait_ge(wu_in, 16)
                act.activation(wu_hi[:, cols], wu_raw[:, cols], ACT.Copy).then_inc(w_hi_done, 1)

            def constants():
                act.wait_ge(attn_w_in, 6 * 16)
                act.activation(ident_bf[:], ident[:], ACT.Copy).then_inc(consts_ready, 1)
                act.activation(mask[:], mask_raw[:], ACT.Copy).then_inc(consts_ready, 1)
                act.mul(wq_scaled[:], wq_raw[:], float(HD) ** -0.5).then_inc(wq_scaled_done, 1)
                act.wait_ge(wq_scaled_done, 1)
                for c in range(4):
                    act.activation(wq_hi[:, c, :].rearrange("p (j r d) -> p j r d", j=4, r=4), q_heads(wq_scaled, c),
                                   ACT.Copy).then_inc(attn_hi_done, 1)
                act.activation(wk_hi[:].rearrange("p (r d) -> p r d", d=HD),
                               wk_raw[:].unsqueeze(1).to_broadcast([P, P // HD, HD]), ACT.Copy).then_inc(attn_hi_done, 1)
                act.activation(wv_parts[:, 0], wv_raw[:], ACT.Copy).then_inc(attn_hi_done, 1)

            def move_x_hi(run):
                wait(act, xt_hi_done, 1, run, 1)
                wait(act, u_psum, CH, run, 0)
                act.activation(xt_hi[:], xt_next_hi[:].bitcast(F32), ACT.Copy).then_inc(xt_moved_hi, 1)

            weights_hi(0)
            move_x_hi(0)
            logits_lo(0, pO)
            gate_exp(0)

            def unit(u, attn, next_attn, last):
                a = u - LAG
                first = isinstance(u, int) and u == 0
                prep = prep_bank(attn)

                def tanh(e):
                    wait(act, g_psum, CH, u, e + 1)
                    wait(act, sg_done, CH, u, e - 1)
                    act.activation(th[:, e % 2], g_bank(attn, e)[:], ACT.Tanh, scale=0.5).then_inc(tanh_done, 1)

                def qk_high(c):
                    wait(act, qk_psum, 5, a, c + 1)
                    wait(act, qk_done, 8, a, max(c - 1, 0))
                    act.activation(qk_hi[:, c % 2, :], (q_banks + [k_bank])[c][:], ACT.Copy).then_inc(qk_hi_done, 1)

                def copy_probs(i, h):
                    wait(act, t_psum, 2 * NBLK, a, 2 * i + h + 1)
                    wait(act, o_psum, NBLK, a, i - 1)
                    act.activation(prob_t[:, i % 2, 4 * h:4 * h + 4, :], pT[:].rearrange("p (s k) -> p s k", s=4),
                                   ACT.Copy).then_inc(t_copied, 1)

                def exps(i, h):
                    wait(act, max_done, 2 * NBLK, a, 2 * i + h + 1)
                    wait(act, t_psum, 2 * NBLK, a, 2 * i + h - 3)
                    for s in range(4 * h, 4 * h + 4):
                        ins = act.activation(prob[:, i % 2, s, :], (pS0, pS1)[h][:, P * (s % 4):P * (s % 4 + 1)],
                                             ACT.Exp, bias=neg_max[:, s:s + 1])
                    ins.then_inc(exp_done, 1)

                def combine_columns():
                    wait(act, comb_psum, 1, u, 1)
                    act.activation(comb_t[:], prep[:], ACT.Copy).then_inc(comb_t_done, 1)

                def copy_y():
                    wait(act, down_done, CH, u, 0)
                    act.activation(y_sb[:], pY[:], ACT.Copy).then_inc(y_copied, 1)

                def output_columns(b, i):
                    wait(act, ot_psum, NBLK, b, i + 1)
                    act.activation(o_t[0:P // 2, :, QB * i:QB * (i + 1)],
                                   pG[0:P // 2, 0:P].rearrange("p (c q) -> p c q", c=2),
                                   ACT.Copy).then_inc(ot_copied, 1)

                for t, e in schedule(attn):
                    if attn and t == 0:
                        if isinstance(u, int):
                            act.wait_ge(zeroed, 9)
                        for c in range(3):
                            qk_high(c)
                    if t == 0 and later_attention(u):
                        output_columns(a - 1, NBLK - 1)
                    if e is not None and (attn or e == 0):
                        tanh(e)
                    if e == 0 and not first:
                        combine_columns()
                    if not attn and e + 1 < CH:
                        tanh(e + 1)
                    if e == CH - 1 and not last:
                        move_x_hi(u + 1)
                    if first and e == 0:
                        act.wait_ge(const_in, 32)
                        act.activation(sel[:], sel_raw[:], ACT.Copy).then_inc(consts_ready, 1)
                        weights_hi(1)
                    if first and e == 0:
                        combine_columns()
                    if t == X_COLUMNS[attn] and not last:
                        next_x(u + 1, prep)
                    if t == XA_COLUMNS[attn] and next_attn:
                        wait(act, xa_psum, 1, u - 1, 1)
                        act.activation(xa_hi[:], prep[:], ACT.Copy).then_inc(xa_hi_done, 1)
                    if not attn and e < NP2:
                        wait(act, c_psum, NP2, u, e + 1)
                        wait(act, hid_done, CH, u, e - 1)
                        act.activation(c_sb[:, e % 2, :], c_bank(attn, e)[:], ACT.Copy).then_inc(c_copied, 1)
                    if first and e == 0:
                        weights_hi(2)
                    if first and e == 4:
                        constants()
                    if attn and t == 0:
                        qk_high(3)
                        qk_high(4)
                        wait(act, v_psum, 1, a, 1)
                        act.activation(v_lo[:], v_bank[:, 0:NBLK * 2 * HD]
                                       .rearrange("p (i h d) -> p i h d", h=2, d=HD)[:, :, 1, :],
                                       ACT.Copy).then_inc(v_lo_done, 1)
                    if attn and 2 <= t < NBLK + 2:
                        copy_probs(t - 2, 0)
                    if attn and 1 <= t < NBLK + 1:
                        exps(t - 1, 0)
                    if attn and 3 <= t < NBLK + 3:
                        wait(act, o_psum, NBLK, a, t - 2)
                        act.activation(o_raw[:], pO[:, 0:BACK], ACT.Copy).then_inc(o_copied, 1)
                    if attn and 4 <= t < NBLK + 3:
                        output_columns(a, t - 4)
                    if attn and 1 <= t < NBLK + 1:
                        exps(t - 1, 1)
                    if t == LOGITS[attn] and not last:
                        logits_lo(u + 1, prep)
                    if attn and 2 <= t < NBLK + 2:
                        copy_probs(t - 2, 1)
                    if t == LOGITS[attn] and not last:
                        gate_exp(u + 1)
                    if t == Y_DONE[attn] and not first:
                        copy_y()

            units(act, unit)
            act.wait_ge(down_done, CH * UNITS)
            act.activation(y_sb[:], pY[:], ACT.Copy).then_inc(y_copied, 1)

        @block.vector
        def _(dve):
            def wait_by_memset(s, per, index, k):
                wait(dve, s, per, index, k)
                if not isinstance(index, int):
                    dve.memset(pause[:], 0.0)

            def layernorm(slot, sems, run):
                s_stats, s_mv, to = sems
                for t in range(NT):
                    dve.bn_stats(stats[:, t, :], X[:, slot, t, :]).then_inc(s_stats, 1)
                wait_by_memset(s_stats, NT, run, NT)
                for t in range(NT):
                    dve.bn_aggr(to[:, t, :], stats[:, t, :]).then_inc(s_mv, 1)

            F_LN = (stats_done, mv_done, mv)
            A_LN = (astats_done, amv_done, amv)

            def route(run, k):
                if k == 1:
                    wait(dve, gate_exp_done, 1, run, 1)
                elif k == 14:
                    wait_by_memset(route_step, ROUTE_STEPS, run, k - 1)
                else:
                    need = {5: 3, 6: 3, 9: 7, 16: 14, 17: 15}.get(k, k - 1)
                    wait(dve, route_step, ROUTE_STEPS, run, need)
                choice = r_choice[:].rearrange("p t (g i) -> p (t g) i", g=GROUPS)
                other = r_group[:].unsqueeze(2).to_broadcast([P, NT, GROUPS, GROUPS])
                own = r_group[:].unsqueeze(3).to_broadcast([P, NT, GROUPS, GROUPS])
                fourth = r_top8[:, :, TOP_K - 1:TOP_K].to_broadcast([P, NT, E])
                if k == 1:
                    ins = dve.tensor_scalar(r_den[:], r_exp[:], 1.0, None, ALU.add)
                elif k == 2:
                    ins = dve.reciprocal(r_score[:], r_den[:])
                elif k == 3:
                    ins = dve.tensor_tensor(r_choice[:], r_score[:],
                                            gbias_sb[:].unsqueeze(1).to_broadcast([P, NT, E]), ALU.add)
                elif k == 4:
                    ins = dve.tensor_tensor(r_pair[:, :, 0:3], choice[:, :, 0:3], choice[:, :, 1:4], ALU.add)
                elif k == 5:
                    ins = dve.tensor_tensor(r_pair[:, :, 3:5], choice[:, :, 0:2], choice[:, :, 2:4], ALU.add)
                elif k == 6:
                    ins = dve.tensor_tensor(r_pair[:, :, 5:6], choice[:, :, 0:1], choice[:, :, 3:4], ALU.add)
                elif k == 7:
                    ins = dve.tensor_reduce(r_group[:].rearrange("p t g -> p (t g)"), r_pair[:], AX.X, ALU.max)
                elif k == 8:
                    ins = dve.tensor_tensor(r_gt[:], other, own, ALU.is_gt)
                elif k == 9:
                    ins = dve.tensor_tensor(r_eq[:], other, own, ALU.is_equal)
                elif k == 10:
                    ins = dve.tensor_tensor(r_eq_tri[:], r_eq[:],
                                            tri[:].unsqueeze(1).to_broadcast([P, NT, GROUPS, GROUPS]), ALU.mult)
                elif k == 11:
                    ins = dve.tensor_tensor(r_before[:], r_gt[:], r_eq_tri[:], ALU.add)
                elif k == 12:
                    ins = dve.tensor_reduce(r_rank[:], r_before[:].rearrange("p t g j -> p (t g) j"), AX.X, ALU.add)
                elif k == 13:
                    ins = dve.scalar_tensor_tensor(r_masked[:].rearrange("p t (g i) -> p (t g) i", g=GROUPS),
                                                   r_rank[:].unsqueeze(2)
                                                   .to_broadcast([P, NT * GROUPS, E // GROUPS]),
                                                   float(TOP_GROUPS), choice, ALU.is_lt, ALU.mult)
                elif k == 14:
                    for t in range(NT):
                        ins = dve.max(r_top8[:, t, :], r_masked[:, t, :])
                elif k == 15:
                    ins = dve.tensor_tensor(r_above[:], r_masked[:], fourth, ALU.is_gt)
                elif k == 16:
                    ins = dve.tensor_tensor(r_tie[:, :, 1:], r_masked[:], fourth, ALU.is_equal)
                elif k == 17:
                    ins = dve.tensor_reduce(r_tie[:, :, 0], r_above[:], AX.X, ALU.add)
                elif k == 18:
                    ins = dve.tensor_tensor_scan(r_count[:].rearrange("p t e -> p (t e)"),
                                                 r_carry[:].rearrange("p t e -> p (t e)"),
                                                 r_tie[:].rearrange("p t e -> p (t e)"), 0.0, ALU.mult, ALU.add)
                elif k == 19:
                    ins = dve.scalar_tensor_tensor(r_tie_in[:], r_count[:, :, 1:], float(TOP_K), r_tie[:, :, 1:],
                                                   ALU.is_le, ALU.mult)
                elif k == 20:
                    ins = dve.tensor_tensor(r_pick[:], r_tie_in[:], r_above[:], ALU.add)
                elif k == 21:
                    ins = dve.tensor_tensor(r_w[:], r_pick[:], r_masked[:], ALU.mult)
                elif k == 22:
                    ins = dve.tensor_reduce(r_sum[:], r_w[:], AX.X, ALU.add)
                elif k == 23:
                    ins = dve.tensor_scalar(r_sum_eps[:], r_sum[:], 1e-20, None, ALU.add)
                elif k == 24:
                    ins = dve.reciprocal(r_inv[:], r_sum_eps[:])
                elif k == 25:
                    ins = dve.scalar_tensor_tensor(r_comb[:], r_w[:], ROUTE_SCALE, r_inv[:].unsqueeze(2)
                                                   .to_broadcast([P, NT, E]), ALU.mult, ALU.mult)
                elif k == 26:
                    wait(dve, comb_psum, 1, run, 0)
                    ins = dve.tensor_copy(comb[:, :, 0:E].bitcast(F32R), r_comb[:])
                elif k == 27:
                    ins = dve.tensor_tensor(comb[:, :, E:2 * E].bitcast(F32R), r_comb[:], comb[:, :, 0:E],
                                            ALU.subtract)
                ins.then_inc(route_step, 1)

            def route_part(run, attn, t, m):
                parts = [(tick, n, count) for tick, counts in (ROUTE_ATTN if attn else ROUTE_ALONE).items()
                         for n, count in enumerate(counts)]
                done = sum(count for tick, n, count in parts if (tick, n) < (t, m))
                here = sum(count for tick, n, count in parts if (tick, n) == (t, m))
                for k in range(done + 1, done + here + 1):
                    route(run, k)

            def next_x_lo(run, bank):
                wait(dve, xt_hi_done, 1, run, 1)
                dve.tensor_tensor(xt_next_lo[:], bank[:], xt_next_hi[:].bitcast(F32), ALU.subtract)\
                   .then_inc(xt_lo_done, 1)

            dve.wait_ge(x_in[0], 16)
            layernorm(0, F_LN, 0)
            dve.wait_ge(w_hi_done, 1)
            dve.tensor_tensor(gk_parts[:, 1], gk_raw[:], gk_parts[:, 0].bitcast(F32), ALU.subtract).then_inc(w_lo_done, 1)
            dve.wait_ge(mv_done, NT)
            dve.wait_ge(rstd_done, 1)
            for t in range(NT):
                ins = dve.tensor_scalar(xn[:, t, :], X[:, 0, t, :], mv[:, t, 0:1], rstd[:, t:t + 1],
                                        ALU.subtract, ALU.mult)
            ins.then_inc(xn_done, 1)
            next_x_lo(0, pO)

            def sum_logits(run, bank):
                wait(dve, logits_lo_done, 1, run, 1)
                dve.tensor_tensor(r_logit[:], bank[:, 0:NT * 2 * E].rearrange("p (t h e) -> p t h e", t=NT, h=2)
                                  [:, :, 0, :], r_logit_lo[:], ALU.add).then_inc(logits_done, 1)

            def weights_lo(n):
                cols = slice(n * WPC, (n + 1) * WPC)
                dve.wait_ge(w_hi_done, 2 + 2 * n)
                dve.tensor_tensor(wg_lo[:, cols], wg_raw[:, cols], wg_hi[:, cols].bitcast(F32), ALU.subtract)\
                   .then_inc(w_lo_done, 1)
                dve.wait_ge(w_hi_done, 3 + 2 * n)
                dve.tensor_tensor(wu_lo[:, cols], wu_raw[:, cols], wu_hi[:, cols].bitcast(F32), ALU.subtract)\
                   .then_inc(w_lo_done, 1)

            def move_x_lo(run):
                wait(dve, xt_lo_done, 1, run, 1)
                wait(dve, u_psum, CH, run, 0)
                dve.tensor_copy(xt_lo[:], xt_next_lo[:].bitcast(F32)).then_inc(xt_moved_lo, 1)

            weights_lo(0)
            move_x_lo(0)
            sum_logits(0, pO)

            def unit(u, attn, next_attn, last):
                a = u - LAG
                if isinstance(u, int) and u == 1:
                    dve.wait_ge(zeroed, 9)
                def attention_weights_lo():
                    for c in range(4):
                        dve.wait_ge(attn_hi_done, c + 1)
                        dve.tensor_tensor(wq_lo[:, c, :].rearrange("p (j r d) -> p j r d", j=4, r=4),
                                          q_heads(wq_scaled, c),
                                          wq_hi[:, c, :].bitcast(F32).rearrange("p (j r d) -> p j r d", j=4, r=4),
                                          ALU.subtract).then_inc(attn_lo_done, 1)
                    dve.wait_ge(attn_hi_done, 6)
                    dve.tensor_tensor(wk_lo[:].rearrange("p (r d) -> p r d", d=HD),
                                      wk_raw[:].unsqueeze(1).to_broadcast([P, P // HD, HD]),
                                      wk_hi[:].bitcast(F32).rearrange("p (r d) -> p r d", d=HD), ALU.subtract)\
                       .then_inc(attn_lo_done, 1)
                    dve.tensor_tensor(wv_parts[:, 1], wv_raw[:], wv_parts[:, 0].bitcast(F32), ALU.subtract)\
                       .then_inc(attn_lo_done, 1)

                def q_part(c):
                    wait(dve, qk_hi_done, 5, a, c + 1)
                    dve.scalar_tensor_tensor(q_rep[:, c // 2, :, c % 2, :],
                                             qk_hi[:, c % 2, :].bitcast(F32).rearrange("p (i q) -> p i q", q=QB),
                                             beta[:, 0:1], q_banks[c][:].rearrange("p (i q) -> p i q", q=QB),
                                             ALU.mult, ALU.add).then_inc(qk_done, 1)

                def k_part():
                    wait(dve, qk_hi_done, 5, a, 5)
                    for j in range(4):
                        rows = slice(32 * j, 32 * j + 32)
                        dve.scalar_tensor_tensor(k_diag[rows, j, :], qk_hi[rows, 0, :].bitcast(F32), beta[rows, 1:2],
                                                 k_bank[rows, :], ALU.mult, ALU.add).then_inc(qk_done, 1)

                def chunk_gate(e):
                    wait(dve, tanh_done, CH, u, e + 1)
                    dve.scalar_tensor_tensor(sg[:, e % 2, :], th[:, e % 2], 1.0, g_bank(attn, e)[:], ALU.add, ALU.mult)\
                       .then_inc(sg_done, 1)

                def chunk_up(e):
                    wait(dve, sg_done, CH, u, e + 1)
                    wait(dve, u_psum, CH, u, e + 1)
                    up = u_bank(attn, e)
                    if e == CH - 1:
                        if not attn:
                            wait(dve, hid_done, CH, u, e)
                        wait(dve, down_done, CH, u, e - HIDS + 1)
                        dve.scalar_tensor_tensor(hid[:, e % HIDS, :], sg[:, e % 2, :], 0.5, up[:], ALU.mult, ALU.mult)\
                           .then_inc(hid_done, 1)
                    else:
                        wait(dve, hid_done, CH, u, e - 1)
                        dve.scalar_tensor_tensor(gu[:, e % 2, :], sg[:, e % 2, :], 0.5, up[:], ALU.mult, ALU.mult)\
                           .then_inc(gu_done, 1)

                def chunk_weight(e):
                    wait(dve, gu_done, NP2, u, e + 1)
                    wait(dve, c_psum, NP2, u, e + 1)
                    wait(dve, down_done, CH, u, e - HIDS + 1)
                    dve.tensor_tensor(hid[:, e % HIDS, :], gu[:, e % 2, :], c_bank(attn, e)[:], ALU.mult)\
                       .then_inc(hid_done, 1)

                def negated_max(i, h):
                    wait(dve, s_psum, 2 * NBLK, a, 2 * i + h + 1)
                    wait(dve, exp_done, 2 * NBLK, a, 2 * i + h - 1)
                    dve.tensor_reduce(neg_max[:, 4 * h:4 * h + 4], (pS0, pS1)[h][:].rearrange("p (s k) -> p s k", s=4),
                                      AX.X, ALU.max, negate=True).then_inc(max_done, 1)

                def next_layernorm():
                    if isinstance(u, int) and u + 1 < NB:
                        dve.wait_ge(x_in[u + 1], 16)
                    else:
                        wait_apart(dve, attn_added, 1, u, 2 - NB)
                    layernorm(u + 1, F_LN, u + 1)

                first = isinstance(u, int) and u == 0
                prep = prep_bank(attn)
                for t, e in schedule(attn):
                    if attn and t == 0:
                        if isinstance(u, int):
                            dve.wait_ge(zeroed, 9)
                        q_part(0)
                        q_part(1)
                        q_part(2)
                    if attn and 1 <= t < NBLK + 1:
                        negated_max(t - 1, 0)
                    if e == 0 and later_attention(u):
                        wait(dve, attn_psum, 1, a, 0)
                        dve.tensor_tensor(X[:, u - 1 - LAG + NB].rearrange("p t d -> p (t d)"), pS0[:],
                                          X[:, u - 1 - LAG].rearrange("p t d -> p (t d)"), ALU.add)\
                           .then_inc(attn_added, 1)
                    if first and e == 0:
                        dve.wait_ge(zeroed, 5)
                        dve.wait_ge(const_in, 32)
                        dve.wait_ge(route_in, 32)
                        for k in range(1, 10):
                            route(0, k)
                    if t == X_NORM[attn] and not (attn or first or last):
                        next_layernorm()
                    if e is not None:
                        chunk_gate(e)
                    if e == CH - 1 and not last:
                        move_x_lo(u + 1)
                    if not last:
                        route_part(u + 1, attn, t, 0)
                    if first and e == 0:
                        for k in range(10, 19):
                            route(0, k)
                    if e is not None:
                        chunk_up(e)
                    if t == X_COLUMNS[attn] and not last:
                        next_x_lo(u + 1, prep)
                    if t == XA_COLUMNS[attn] and next_attn:
                        wait(dve, xa_hi_done, 1, u - 1, 1)
                        dve.tensor_tensor(xa_lo[:], prep[:], xa_hi[:].bitcast(F32), ALU.subtract)\
                           .then_inc(xa_lo_done, 1)
                    if not last:
                        route_part(u + 1, attn, t, 1)
                    if first and e == 0:
                        for k in range(19, ROUTE_STEPS + 1):
                            route(0, k)
                    if attn and t == 0:
                        q_part(3)
                        k_part()
                        wait(dve, v_lo_done, 1, a, 1)
                        wait(dve, o_psum, NBLK, a, 0)
                        dve.tensor_tensor(v_one[:, :, 0:HD], v_bank[:, 0:NBLK * 2 * HD]
                                          .rearrange("p (i h d) -> p i h d", h=2, d=HD)[:, :, 0, :], v_lo[:],
                                          ALU.add).then_inc(v_done, 1)
                    if attn and 1 <= t < NBLK + 1:
                        negated_max(t - 1, 1)
                    if t == Y_ROWS[attn] and not first:
                        wait(dve, y_back, 1, u, 0)
                        dve.scalar_tensor_tensor(X[:, u - 1].rearrange("p t d -> p (t d)"), pO[:], 0.5,
                                                 X[:, u - 1].rearrange("p t d -> p (t d)"), ALU.mult, ALU.add)\
                           .then_inc(x_added, 1)
                    if attn and e is not None and e < NP2:
                        chunk_weight(e)
                    o_all = pO[:, BACK:2 * BACK].rearrange("p (s r) -> p s r", r=32)
                    if attn and 3 <= t < NBLK + 3:
                        wait(dve, back_psum, NBLK, a, t - 2)
                        dve.reciprocal(o_inv[:], o_all[:, :, HD]).then_inc(o_inv_done, 1)
                    if not last:
                        route_part(u + 1, attn, t, 2)
                    if attn and 3 <= t < NBLK + 3:
                        wait(dve, o_inv_done, NBLK, a, t - 2)
                        wait(dve, ot_psum, NBLK, a, t - 3)
                        dve.tensor_tensor(o_norm[:], o_all[:, :, 0:HD], o_inv[:].unsqueeze(2)
                                          .to_broadcast([P, 8, HD]), ALU.mult).then_inc(o_norm_done, 1)
                    if t == LOGITS[attn] and not last:
                        sum_logits(u + 1, prep)
                    if first and e == 0:
                        weights_lo(1)
                    if first and e == 1:
                        weights_lo(2)
                    if isinstance(u, int) and u == 1 and e == 2:
                        attention_weights_lo()
                    if t == X_NORM[attn] and (attn or first):
                        next_layernorm()
                    if t == XA_NORM[attn] and next_attn:
                        wait_apart(dve, x_added, 1, u, 0)
                        layernorm(u - 1, A_LN, u - 1)

            units(dve, unit)
            dve.wait_ge(y_back, UNITS)
            dve.scalar_tensor_tensor(X[:, UNITS - 1].rearrange("p t d -> p (t d)"), pO[:], 0.5,
                                     X[:, UNITS - 1].rearrange("p t d -> p (t d)"), ALU.mult, ALU.add)\
               .then_inc(x_added, 1)

        @block.tensor
        def _(pe):
            def three(dst, w_hi, w_lo, x_hi, x_lo, start=True):
                pe.matmul(dst, w_hi, x_hi, start=start, stop=False)
                pe.matmul(dst, w_lo, x_hi, start=False, stop=False)
                return pe.matmul(dst, w_hi, x_lo, start=False, stop=True)

            def to_columns(bank, done, xn_sem, run):
                wait(pe, xn_sem, 1, run, 1)
                for t in range(NT):
                    ins = pe.transpose(bank[:, P * t:P * (t + 1)], xn[:, t, :], ident[:])
                ins.then_inc(done, 1)

            def logits(run, bank):
                wait(pe, xt_hi_done, 1, run, 1)
                wait(pe, xt_lo_done, 1, run, 1)
                for t in range(NT):
                    tok = slice(P * t, P * (t + 1))
                    dst = bank[:, 2 * E * t:2 * E * (t + 1)]
                    parts = gk_parts[:].rearrange("p h e -> p (h e)")
                    pe.matmul(dst, xt_next_hi[:, tok], parts, start=True, stop=False)
                    ins = pe.matmul(dst, xt_next_lo[:, tok], parts, start=False, stop=True)
                ins.then_inc(logits_psum, 1)

            def down(n, e, first_unit=False):
                wait(pe, hid_done, CH, n, e + 1)
                if e == 0:
                    wait(pe, y_copied, 1, n, 0)
                if first_unit and e == 0:
                    pe.wait_ge(wd_in, 16)
                pe.matmul(pY[:], wd_sb[:, e, :], hid[:, e % HIDS, :], start=(e == 0), stop=(e == CH - 1))\
                  .then_inc(down_done, 1)

            def y_to_rows(n, bank):
                wait(pe, y_copied, 1, n, 1)
                wait(pe, x_added, 1, n, 0)
                for s in range(NT):
                    ins = pe.transpose(bank[:, P * s:P * (s + 1)], y_sb[:, P * s:P * (s + 1)], ident[:])
                ins.then_inc(y_back, 1)

            pe.wait_ge(zeroed, 5)
            for _ in range(3):
                pe.matmul(pY[:], comb[:, 0, :], comb[:].rearrange("p t k -> p (t k)"), start=True, stop=True)
            pe.wait_ge(ident_loaded, 16)
            to_columns(pO, xt_psum, xn_done, 0)
            pe.wait_ge(w_hi_done, 1)
            pe.wait_ge(w_lo_done, 1)
            logits(0, pO)

            def unit(u, attn, next_attn, last):
                a = u - LAG
                first = isinstance(u, int) and u == 0
                prep = prep_bank(attn)

                def gate(t, e):
                    if attn and t >= 5:
                        wait(pe, ot_copied, NBLK, a, t - 4)
                    if e == 0:
                        wait(pe, xt_moved_hi, 1, u, 1)
                        wait(pe, xt_moved_lo, 1, u, 1)
                        wait(pe, sg_done, CH, u, 0)
                        wait(pe, hid_done, CH, u, 0)
                    if first:
                        n = (P * (e + 1) - 1) // WPC
                        pe.wait_ge(w_lo_done, 3 + 2 * n)
                    if e == 1 and isinstance(u, int) and u == LAG + NB:
                        pe.wait_ge(attn_added, NB)
                    cols = slice(P * e, P * (e + 1))
                    before = e if attn else e - 1
                    if e > 0:
                        wait(pe, sg_done, CH, u, before)
                    three(g_bank(attn, e)[:], wg_hi[:, cols], wg_lo[:, cols], xt_hi[:], xt_lo[:]).then_inc(g_psum, 1)

                def up(e):
                    cols = slice(P * e, P * (e + 1))
                    if e > 0:
                        wait(pe, gu_done, NP2, u, e if attn else e - 1)
                    three(u_bank(attn, e)[:], wu_hi[:, cols], wu_lo[:, cols], xt_hi[:], xt_lo[:]).then_inc(u_psum, 1)

                def combine(e):
                    if e == 0:
                        wait(pe, comb_t_done, 1, u, 1)
                        if first:
                            pe.wait_ge(consts_ready, 1)
                    elif attn:
                        wait(pe, hid_done, CH, u, e)
                        if e == CHUNK_TICKS.index(LOGITS[attn] + 1):
                            wait(pe, logits_done, 1, u + 1, 1)
                        if e == CHUNK_TICKS.index(XA_COLUMNS[attn] + 1) and next_attn:
                            wait(pe, xa_lo_done, 1, u - 1, 1)
                    else:
                        wait(pe, c_copied, NP2, ALONE[u], e - 1)
                    pe.matmul(c_bank(attn, e)[:], sel[:, e, :], comb_t[:], start=True, stop=True).then_inc(c_psum, 1)

                def combine_to_columns():
                    wait(pe, route_step, ROUTE_STEPS, u, ROUTE_STEPS)
                    if attn:
                        wait(pe, hid_done, CH, u, -1)
                    for s in range(NT):
                        ins = pe.transpose(prep[:, P * s:P * (s + 1)], comb[:, s, :], ident[:])
                    ins.then_inc(comb_psum, 1)

                def columns(t):
                    if t == X_COLUMNS[attn] and not last:
                        if attn:
                            wait(pe, hid_done, CH, u, t)
                        else:
                            wait(pe, comb_t_done, 1, u, 1)
                            wait(pe, x_added, 1, u, 0)
                        to_columns(prep, xt_psum, xn_done, u + 1)
                    if t == XA_COLUMNS[attn] and next_attn:
                        if attn:
                            wait(pe, hid_done, CH, u, t - 1)
                        wait(pe, logits_done, 1, u + 1, 1)
                        to_columns(prep, xa_psum, axn_done, u - 1)

                def transpose_probs(i, h):
                    wait(pe, exp_done, 2 * NBLK, a, 2 * i + h + 1)
                    wait(pe, t_copied, 2 * NBLK, a, 2 * i + h)
                    if i == 0 and h == 0:
                        wait(pe, v_done, 1, a, 1)
                    for s in range(4):
                        ins = pe.transpose(pT[:, P * s:P * (s + 1)], prob[:, i % 2, 4 * h + s, :], ident[:])
                    ins.then_inc(t_psum, 1)

                def weighted_values(i):
                    wait(pe, t_copied, 2 * NBLK, a, 2 * i + 2)
                    wait(pe, o_norm_done, NBLK, a, i)
                    if i == 0:
                        wait(pe, x_added, 1, u, 0)
                    for j in range(4):
                        ins = pe.matmul(pO[32 * j:32 * j + 32, 0:BACK], v_one[:, i, :],
                                        prob_t[:, i % 2].rearrange("p (h j) q -> p j h q", h=2)[:, j, :, :],
                                        start=True, stop=True)
                    ins.then_inc(o_psum, 1)

                def gate_bank_free(b, i, gates):
                    wait(pe, sg_done, CH, u, gates)
                    wait(pe, ot_copied, NBLK, b, i)

                def output_to_rows(i):
                    wait(pe, o_copied, NBLK, a, i + 1)
                    for h in range(2):
                        ins = pe.transpose(pO[:, BACK + P * h:BACK + P * (h + 1)], o_raw[:, P * h:P * (h + 1)],
                                           ident[:])
                    ins.then_inc(back_psum, 1)

                def output_to_columns(b, i):
                    wait_apart(pe, o_norm_done, NBLK, b, i + 1)
                    pe.transpose(pG[0:P // 2, 0:P], o_norm[:].rearrange("p s d -> p (s d)"), ident[:])\
                      .then_inc(ot_psum, 1)

                def scores(i, h):
                    if i == 0 and h == 0:
                        wait(pe, qk_done, 8, a, 8)
                    ks = key_start(i)
                    bank = (pS0, pS1)[h]
                    wait(pe, exp_done, 2 * NBLK, a, 2 * i + h - 1)
                    pe.matmul(bank[:], ident_bf[:], mask[:, mask_kind(i):mask_kind(i) + 1, :]
                              .to_broadcast([P, 4, P]), start=True, stop=False)
                    pe.matmul(bank[:], q_rep[:, h, i, :, :].rearrange("p c q -> p (c q)"),
                              k_diag[:, :, ks:ks + P], start=False, stop=True).then_inc(s_psum, 1)

                def project():
                    wait(pe, ot_copied, NBLK, a, 0)
                    wait(pe, exp_done, 2 * NBLK, a, 0)
                    for s in range(NT):
                        tok = slice(P * s, P * (s + 1))
                        dst = pS0[:, P * s:P * (s + 1)]
                        pe.matmul(dst, o_t[:, 0, tok], wf_sb[:, 0, :], start=True, stop=False)
                        ins = pe.matmul(dst, o_t[:, 1, tok], wf_sb[:, 1, :], start=False, stop=True)
                    ins.then_inc(attn_psum, 1)

                for t, e in schedule(attn):
                    if attn and t == 0:
                        if isinstance(u, int):
                            pe.wait_ge(attn_lo_done, 6)
                            pe.wait_ge(consts_ready, 3)
                            pe.wait_ge(zeroed, 9)
                            pe.wait_ge(hid_done, CH * u - 1)
                        wait(pe, xa_hi_done, 1, a, 1)
                        wait(pe, xa_lo_done, 1, a, 1)
                        wait(pe, exp_done, 2 * NBLK, a, 0)
                        wait(pe, t_copied, 2 * NBLK, a, 0)
                        for c in range(3):
                            if c == 2:
                                wait(pe, o_norm_done, NBLK, a, 0)
                                gate_bank_free(a, -1, 0)
                            three(q_banks[c][:], wq_hi[:, c, :], wq_lo[:, c, :], xa_hi[:], xa_lo[:])\
                                .then_inc(qk_psum, 1)
                    if t == 0 and later_attention(u):
                        if not attn:
                            gate_bank_free(a, -1, 0)
                        output_to_columns(a, -1)
                    if e == 0 and not first:
                        down(u - 1, CH - 2)
                    if t == 0 and later_attention(u):
                        project()
                    if e is not None and (attn or e == 0):
                        gate(t, e)
                    if attn and 1 <= t < NBLK + 1:
                        scores(t - 1, 0)
                    if e is not None and (attn or e == 0):
                        up(e)
                    if e == 0 and not first:
                        combine_to_columns()
                    if not attn and e + 1 < CH:
                        gate(t, e + 1)
                        up(e + 1)
                    if first and e == 0:
                        combine_to_columns()
                    columns(t)
                    if attn and 2 <= t < NBLK + 2:
                        transpose_probs(t - 2, 0)
                    if attn and 1 <= t < NBLK + 1:
                        scores(t - 1, 1)
                    if attn and 3 <= t < NBLK + 3:
                        weighted_values(t - 3)
                    if attn and t == 0:
                        wait(pe, attn_added, 1, a, 0)
                        three(q_banks[3][:], wq_hi[:, 3, :], wq_lo[:, 3, :], xa_hi[:], xa_lo[:])\
                            .then_inc(qk_psum, 1)
                        wait(pe, qk_done, 8, a, 1)
                        three(k_bank[:], wk_hi[:], wk_lo[:], xa_hi[:], xa_lo[:]).then_inc(qk_psum, 1)
                        wait(pe, qk_done, 8, a, 2)
                        for i in range(NBLK):
                            keys = slice(key_start(i), key_start(i) + P)
                            dst = v_bank[:, 2 * HD * i:2 * HD * (i + 1)]
                            parts = wv_parts[:].rearrange("p h d -> p (h d)")
                            pe.matmul(dst, xa_hi[:, keys], parts, start=True, stop=False)
                            ins = pe.matmul(dst, xa_lo[:, keys], parts, start=False, stop=True)
                        ins.then_inc(v_psum, 1)
                    if t == Y_ROWS[attn] and not first:
                        if not attn:
                            wait(pe, comb_t_done, 1, u, 1)
                        y_to_rows(u - 1, pO)
                    if e is not None and e < NP2:
                        combine(e)
                    if t == Y_DONE[attn] and not first:
                        down(u - 1, CH - 1)
                    if e is not None and e >= 2:
                        down(u, e - 2, first)
                    if attn and 3 <= t < NBLK + 3:
                        if t >= 4:
                            gate_bank_free(a, t - 4, e + 1 if e is not None else CHUNK_TICKS.index(t - 1) + 1)
                        output_to_rows(t - 3)
                    if attn and 4 <= t < NBLK + 3:
                        output_to_columns(a, t - 4)
                    if t == LOGITS[attn] and not last:
                        logits(u + 1, prep)
                    if attn and 2 <= t < NBLK + 2:
                        transpose_probs(t - 2, 1)

            units(pe, unit)
            down(UNITS - 1, CH - 2)
            down(UNITS - 1, CH - 1)
            y_to_rows(UNITS - 1, pO)


def kernel(**inputs):
    import numpy as np
    import concourse.bacc as bacc
    from concourse.bass_utils import run_bass_kernel_spmd

    def a(name):
        return np.asarray(inputs[name])

    def put(z):
        return np.ascontiguousarray(z)

    wg = np.concatenate([a("L0_ffn_w_gate").transpose(1, 0, 2).reshape(D, E * M), a("L0_ffn_sw_gate")], 1)
    wu = np.concatenate([a("L0_ffn_w_up").transpose(1, 0, 2).reshape(D, E * M), a("L0_ffn_sw_up")], 1)
    wd = np.concatenate([a("L0_ffn_w_down").reshape(NP2, P, D), a("L0_ffn_sw_down")[None]], 0).transpose(1, 0, 2)
    q = np.arange(P)[:, None] % QB
    k = np.arange(P)[None, :]
    first_key = [0, -WINDOW, -QB]
    mask = np.stack([np.where(np.abs(q - (k + s)) <= WINDOW, 0.0, -1e30) for s in first_key], 1).astype(np.float32)
    sel = np.zeros((P, NP2, P), np.float32)
    for e in range(E):
        sel[[e, E + e], e // 2, (e % 2) * M:(e % 2 + 1) * M] = 1.0
    tri = np.broadcast_to(np.tril(np.ones((GROUPS, GROUPS), np.float32), -1), (P, GROUPS, GROUPS))
    part = np.arange(P) // HD % 4
    beta = np.stack([np.where(part >= 2, -1.0, 0.0), np.where(part % 2 == 1, -1.0, 0.0)], 1).astype(np.float32)
    arrays = {
        "x": put(a("L0_attn_x").reshape(NB * SEQ, D)), "wg": put(wg), "wu": put(wu), "wd": put(wd),
        "gk": put(a("L0_ffn_gate_kernel")), "gbias": put(np.broadcast_to(a("L0_ffn_gate_bias"), (P, E))),
        "wq": put(a("L0_attn_Wq").T), "wk": put(a("L0_attn_Wk").T), "wv": put(a("L0_attn_Wv").T),
        "wf": put(np.concatenate([a("L0_attn_Wf").T.reshape(2, P // 2, D).transpose(1, 0, 2),
                                  np.stack([a("L0_attn_bf"), np.zeros_like(a("L0_attn_bf"))])[None]], 0)),
        "ident_in": np.eye(P, dtype=np.float32), "mask_in": put(mask), "sel_in": sel, "tri_in": put(tri),
        "beta_in": put(beta),
    }
    nc = bacc.Bacc("TRN2", target_bir_lowering=False, num_devices=1)
    args = [nc.dram_tensor(n, z.shape, mybir.dt.from_np(z.dtype), kind="ExternalInput").ap()
            for n, z in arrays.items()]
    out = nc.dram_tensor("out", (NB * SEQ, D), F32, kind="ExternalOutput").ap()
    macaron(nc, *args, out)
    r = run_bass_kernel_spmd(nc, [arrays], core_ids=[0])
    return r.results[0]["out"].reshape(NB, SEQ, D)
```

```python
from contextlib import ExitStack

import concourse.bass as bass
from concourse import mybir

ALU = mybir.AluOpType
ACT = mybir.ActivationFunctionType
AX = mybir.AxisListType
F32 = mybir.dt.float32
F32R = mybir.dt.float32r
BF16 = mybir.dt.bfloat16

P = 128
NB, SEQ, D = 4, 512, 128
NT = SEQ // P
E, M = 16, 64
CH = E * M // P + 1
NP2 = CH - 1
GROUPS, TOP_GROUPS, TOP_K, ROUTE_SCALE = 4, 2, 4, 2.5
HD, WINDOW = 8, 32
QB = 64
NBLK = SEQ // QB
EPS = 1e-5
UNITS = 2 * NB
LAG = 2

TICKS = NBLK + 3
CHUNK_TICKS = [0, 1, 2, 3, 5, 6, 7, 9, 10]
X_COLUMNS = {True: 4, False: 2}
LOGITS = {True: 4, False: 3}
XA_COLUMNS = {True: 8, False: 6}
Y_DONE = {True: 1, False: 0}
Y_ROWS = {True: 2, False: 1}
X_ADD = {True: 3, False: 1}
X_NORM = {True: 0, False: 0}
XA_NORM = {True: 4, False: 3}
DOWNS = {True: {3: 0, 4: 1, 5: 2, 6: 3, 7: 4, 8: 5, 9: 6}, False: {e: e - 2 for e in range(2, CH)}}
HIDS = 5
ROUTE_STEPS = 27
ROUTE_ATTN = {5: (1, 2, 2), 6: (1, 2, 2), 7: (1, 2, 2), 8: (2, 2, 2), 9: (1, 1, 1), 10: (1, 1, 1)}
ROUTE_ALONE = {4: (1, 2, 2), 5: (1, 2, 2), 6: (2, 2, 2), 7: (1, 2, 2), 8: (2, 2, 2)}
ALONE = {0: 0, 1: 1, UNITS - 2: 2, UNITS - 1: 3}


def key_start(i):
    return min(max(QB * i - WINDOW, 0), SEQ - P)


def mask_kind(i):
    return 0 if i == 0 else 2 if i == NBLK - 1 else 1


def macaron(nc, x, wg, wu, wd, gk, gbias, wq, wk, wv, wf, ident_in, mask_in, sel_in, tri_in, beta_in, out):
    ctx = ExitStack()
    with ctx:
        def sb(name, shape, dt=F32):
            return ctx.enter_context(nc.sbuf_tensor(name, shape, dt))

        def ps(name, shape):
            return ctx.enter_context(nc.psum_tensor(name, shape, F32))

        def sem(name):
            return ctx.enter_context(nc.semaphore(name))

        X = sb("X", [P, UNITS, NT, D])
        wg_raw = sb("wg_raw", [P, CH * P])
        wu_raw = sb("wu_raw", [P, CH * P])
        wg_hi, wg_lo = sb("wg_hi", [P, CH * P], F32R), sb("wg_lo", [P, CH * P], F32R)
        wu_hi, wu_lo = sb("wu_hi", [P, CH * P], F32R), sb("wu_lo", [P, CH * P], F32R)
        wd_sb = sb("wd_sb", [P, CH, D])
        wd_hi, wd_lo = sb("wd_hi", [P, CH, D], F32R), sb("wd_lo", [P, CH, D], F32R)
        gk_raw = sb("gk_raw", [P, E])
        gk_parts = sb("gk_parts", [P, 2, E], F32R)
        gbias_sb = sb("gbias_sb", [P, E])
        wq_raw = sb("wq_raw", [P, D])
        wq_scaled = sb("wq_scaled", [P, D])
        wk_raw = sb("wk_raw", [P, HD])
        wv_raw = sb("wv_raw", [P, HD])
        wq_hi, wq_lo = sb("wq_hi", [P, 4, P], F32R), sb("wq_lo", [P, 4, P], F32R)
        wk_hi, wk_lo = sb("wk_hi", [P, P], F32R), sb("wk_lo", [P, P], F32R)
        wv_parts = sb("wv_parts", [P, 2, HD], F32R)
        v_lo = sb("v_lo", [P, NBLK, HD])
        wf_sb = sb("wf_sb", [P // 2 + 1, 2, D])
        ident = sb("ident", [P, P])
        ident_bf = sb("ident_bf", [P, P], BF16)
        mask_raw = sb("mask_raw", [P, 3, P])
        mask = sb("mask", [P, 3, P], BF16)
        sel_raw = sb("sel_raw", [P, NP2, P])
        sel = sb("sel", [P, NP2, P], F32R)
        tri = sb("tri", [P, GROUPS, GROUPS])
        beta = sb("beta", [P, 2])
        half = sb("half", [P, NT])
        eps = sb("eps", [P, NT])
        one = sb("one", [P, 1])
        pause = sb("pause", [P, 1])

        stats = sb("stats", [P, NT, 6])
        mv = sb("mv", [P, NT, 2])
        amv = sb("amv", [P, NT, 2])
        var_eps = sb("var_eps", [P, NT])
        rstd = sb("rstd", [P, NT])
        x_centred = sb("x_centred", [P, NT, D])
        xn = sb("xn", [P, NT, D])
        xt_next_hi, xt_next_lo = sb("xt_next_hi", [P, SEQ], F32R), sb("xt_next_lo", [P, SEQ], F32R)
        xt_hi, xt_lo = sb("xt_hi", [P, SEQ], F32R), sb("xt_lo", [P, SEQ], F32R)
        xa_hi, xa_lo = sb("xa_hi", [P, SEQ], F32R), sb("xa_lo", [P, SEQ], F32R)
        r_exp = sb("r_exp", [P, NT, E])
        r_logit_lo = sb("r_logit_lo", [P, NT, E])
        r_logit = sb("r_logit", [P, NT, E])
        r_den = sb("r_den", [P, NT, E])
        r_score = sb("r_score", [P, NT, E])
        r_choice = sb("r_choice", [P, NT, E])
        r_pair = sb("r_pair", [P, NT * GROUPS, 6])
        r_group = sb("r_group", [P, NT, GROUPS])
        r_gt = sb("r_gt", [P, NT, GROUPS, GROUPS])
        r_eq = sb("r_eq", [P, NT, GROUPS, GROUPS])
        r_eq_tri = sb("r_eq_tri", [P, NT, GROUPS, GROUPS])
        r_before = sb("r_before", [P, NT, GROUPS, GROUPS])
        r_rank = sb("r_rank", [P, NT * GROUPS])
        r_masked = sb("r_masked", [P, NT, E])
        r_top8 = sb("r_top8", [P, NT, 8])
        r_above = sb("r_above", [P, NT, E])
        r_tie = sb("r_tie", [P, NT, 1 + E])
        r_carry = sb("r_carry", [P, NT, 1 + E])
        r_count = sb("r_count", [P, NT, 1 + E])
        r_tie_in = sb("r_tie_in", [P, NT, E])
        r_pick = sb("r_pick", [P, NT, E])
        r_w = sb("r_w", [P, NT, E])
        r_sum = sb("r_sum", [P, NT])
        r_sum_eps = sb("r_sum_eps", [P, NT])
        r_inv = sb("r_inv", [P, NT])
        r_comb = sb("r_comb", [P, NT, E])
        comb = sb("comb", [P, NT, P])
        comb_t = sb("comb_t", [P, SEQ], F32R)

        th = sb("th", [P, 2, SEQ])
        sg = sb("sg", [P, 2, SEQ])
        gu = sb("gu", [P, 2, SEQ])
        c_sb = sb("c_sb", [P, 2, SEQ])
        hid = sb("hid", [P, HIDS, SEQ])
        hid_hi, hid_lo = sb("hid_hi", [P, HIDS, SEQ], F32R), sb("hid_lo", [P, HIDS, SEQ], F32R)
        y_sb = sb("y_sb", [P, SEQ])

        qk_hi = sb("qk_hi", [P, 2, SEQ], F32R)
        q_rep = sb("q_rep", [P, 2, NBLK, 2, QB], F32R)
        k_all = sb("k_all", [P, SEQ], F32R)
        k_diag = sb("k_diag", [P, 4, SEQ], F32R)
        v_one = sb("v_one", [P, NBLK, 32])
        neg_max = sb("neg_max", [P, 8])
        prob = sb("prob", [P, 2, 8, P])
        prob_t = sb("prob_t", [P, 2, 8, P])
        o_inv = sb("o_inv", [P, 8])
        o_norm = sb("o_norm", [P, 8, HD])
        o_raw = sb("o_raw", [P, 2 * P])
        o_t = sb("o_t", [P // 2 + 1, 2, SEQ])

        pG, pU, pA, pY = ps("pG", [P, SEQ]), ps("pU", [P, SEQ]), ps("pA", [P, SEQ]), ps("pY", [P, SEQ])
        pS0, pS1, pT, pO = ps("pS0", [P, SEQ]), ps("pS1", [P, SEQ]), ps("pT", [P, SEQ]), ps("pO", [P, SEQ])
        BACK = 2 * P
        qk_banks = [pS1, pT, pO, pS1, pS0]
        k_bank, v_bank = pS1, pT

        x_in = [sem(f"x_in{b}") for b in range(NB)]
        ident_loaded, const_in, wg_in, wu_in, wd_in, attn_w_in, route_in, out_done = (
            sem(n) for n in ("ident_loaded", "const_in", "wg_in", "wu_in", "wd_in", "attn_w_in", "route_in", "out_done"))
        zeroed, consts_ready = sem("zeroed"), sem("consts_ready")
        w_hi_done, w_lo_done, w_lo_late = sem("w_hi_done"), sem("w_lo_done"), sem("w_lo_late")
        wq_scaled_done, attn_hi_done, attn_lo_done = sem("wq_scaled_done"), sem("attn_hi_done"), sem("attn_lo_done")
        stats_done, mv_done, eps_done, rstd_done, centred_done, xn_done = (
            sem(n) for n in ("stats_done", "mv_done", "eps_done", "rstd_done", "centred_done", "xn_done"))
        astats_done, amv_done, aeps_done, arstd_done, acentred_done, axn_done = (
            sem(n) for n in ("astats_done", "amv_done", "aeps_done", "arstd_done", "acentred_done", "axn_done"))
        xt_psum, xt_hi_done, xt_lo_done = sem("xt_psum"), sem("xt_hi_done"), sem("xt_lo_done")
        xa_psum, xa_hi_done, xa_lo_done = sem("xa_psum"), sem("xa_hi_done"), sem("xa_lo_done")
        logits_psum, logits_lo_done, logits_done = sem("logits_psum"), sem("logits_lo_done"), sem("logits_done")
        gate_exp_done, route_step = sem("gate_exp_done"), sem("route_step")
        comb_psum, comb_t_done = sem("comb_psum"), sem("comb_t_done")
        xt_moved_hi, xt_moved_lo = sem("xt_moved_hi"), sem("xt_moved_lo")
        g_psum, u_psum, c_psum = sem("g_psum"), sem("u_psum"), sem("c_psum")
        tanh_done, sg_done, gu_done, hid_done, down_done = (
            sem(n) for n in ("tanh_done", "sg_done", "gu_done", "hid_done", "down_done"))
        c_copied = sem("c_copied")
        wd_hi_done, wd_lo_done, hid_hi_done, hid_lo_done = (
            sem(n) for n in ("wd_hi_done", "wd_lo_done", "hid_hi_done", "hid_lo_done"))
        y_copied, y_back, x_added = sem("y_copied"), sem("y_back"), sem("x_added")
        qk_psum, qk_hi_done, qk_done, k_diag_done, v_psum, v_lo_done, v_done = (
            sem(n) for n in ("qk_psum", "qk_hi_done", "qk_done", "k_diag_done", "v_psum", "v_lo_done", "v_done"))
        s_psum, max_done, exp_done, t_psum, t_copied = (
            sem(n) for n in ("s_psum", "max_done", "exp_done", "t_psum", "t_copied"))
        o_psum, o_copied, back_psum, o_inv_done, o_norm_done, ot_psum, ot_copied = (
            sem(n) for n in ("o_psum", "o_copied", "back_psum", "o_inv_done", "o_norm_done", "ot_psum", "ot_copied"))
        attn_psum, attn_added = sem("attn_psum"), sem("attn_added")

        WGP = 3
        WPC = CH * P // WGP

        def g_bank(attn, e):
            return pS0 if not attn and e % 2 else pG

        def u_bank(attn, e):
            return pS1 if not attn and e % 2 else pU

        def c_bank(attn, e):
            return pT if not attn and e % 2 else pA

        def prep_bank(attn):
            return pA if attn else pO

        def wait(eng, s, per, index, k):
            n = index * per + k
            if not isinstance(n, int) or n > 0:
                eng.wait_ge(s, n)

        def wait_apart(eng, s, per, index, k):
            if isinstance(index, int):
                wait(eng, s, per, index, k)
            else:
                n = eng.snap(index * per + k)
                eng.wait_ge(zeroed, 10)
                eng.wait_ge(s, n)

        def schedule(attn):
            if attn:
                return [(t, CHUNK_TICKS.index(t) if t in CHUNK_TICKS else None) for t in range(TICKS)]
            return [(t, t) for t in range(CH)]

        def later_attention(u):
            return not isinstance(u, int) or LAG < u <= LAG + NB

        def downs_before(e):
            return e - HIDS + 1 if e >= HIDS else max(c + 1 for c in range(CH) if c % HIDS == e) - CH

        def q_heads(w, c):
            h0 = 8 * (c % 2) + 4 * (c // 2)
            return w[:, HD * h0:HD * (h0 + 4)].rearrange("p (j d) -> p j d", d=HD).unsqueeze(2)\
                .to_broadcast([P, 4, 4, HD])

        def units(eng, unit):
            unit(0, False, False, False)
            unit(1, False, True, False)
            unit(2, True, True, False)
            with eng.Fori(3, 5) as u:
                unit(u, True, True, False)
            unit(5, True, False, False)
            unit(6, False, False, False)
            unit(7, False, False, True)

        block = ctx.enter_context(nc.Block())

        @block.sync
        def _(sp):
            x_t = x.rearrange("(u t p) d -> u p t d", p=P, t=NT)
            out_t = out.rearrange("(u t p) d -> u p t d", p=P, t=NT)
            sp.dma_start(X[:, 0], x_t[0]).then_inc(x_in[0], 16)
            sp.dma_start(ident[:], ident_in).then_inc(ident_loaded, 16)
            sp.dma_start(tri[:], tri_in).then_inc(const_in, 16)
            sp.dma_start(gk_raw[:], gk).then_inc(route_in, 16)
            sp.dma_start(gbias_sb[:], gbias).then_inc(route_in, 16)
            sp.dma_start(wg_raw[:], wg).then_inc(wg_in, 16)
            sp.dma_start(wu_raw[:], wu).then_inc(wu_in, 16)
            sp.dma_start(sel_raw[:], sel_in).then_inc(const_in, 16)
            sp.dma_start(wd_sb[:], wd).then_inc(wd_in, 16)
            for b in range(1, NB):
                sp.dma_start(X[:, b], x_t[b]).then_inc(x_in[b], 16)
            sp.dma_start(mask_raw[:], mask_in).then_inc(attn_w_in, 16)
            sp.dma_start(beta[:], beta_in).then_inc(attn_w_in, 16)
            sp.dma_start(wq_raw[:], wq).then_inc(attn_w_in, 16)
            sp.dma_start(wk_raw[:], wk).then_inc(attn_w_in, 16)
            sp.dma_start(wv_raw[:], wv).then_inc(attn_w_in, 16)
            sp.dma_start(wf_sb[:], wf).then_inc(attn_w_in, 16)
            for u in range(NB, UNITS):
                sp.wait_ge(x_added, u + 1)
                sp.dma_start(out_t[u - NB], X[:, u]).then_inc(out_done, 16)
            sp.wait_ge(out_done, 16 * NB)

        @block.gpsimd
        def _(pool):
            pool.memset(half[:], -0.5).then_inc(zeroed, 1)
            pool.memset(eps[:], EPS).then_inc(zeroed, 1)
            pool.memset(one[:], 1.0).then_inc(zeroed, 1)
            pool.memset(r_carry[:], 1.0).then_inc(zeroed, 1)
            pool.memset(comb[:], 0.0).then_inc(zeroed, 1)
            pool.wait_ge(zeroed, 5)
            pool.memset(r_carry[:, :, 0:1], 0.0).then_inc(zeroed, 1)

            def rstd_of(mv, mv_sem, eps_sem, rstd_sem, run):
                wait(pool, mv_sem, NT, run, NT)
                pool.tensor_tensor(var_eps[:], mv[:, :, 1], eps[:], ALU.add).then_inc(eps_sem, 1)
                wait(pool, eps_sem, 1, run, 1)
                pool.tensor_tensor(rstd[:], var_eps[:], half[:], ALU.pow).then_inc(rstd_sem, 1)

            pool.wait_ge(zeroed, 2)
            rstd_of(mv, mv_done, eps_done, rstd_done, 0)
            pool.memset(v_one[:], 0.0).then_inc(zeroed, 1)
            pool.memset(k_diag[:].bitcast(F32), 0.0).then_inc(zeroed, 1)
            pool.wait_ge(zeroed, 8)
            pool.memset(o_t[P // 2:P // 2 + 1, :, :], 1.0).then_inc(zeroed, 1)
            pool.wait_ge(zeroed, 9)
            pool.memset(v_one[:, :, HD:HD + 1], 1.0).then_inc(zeroed, 1)

            for n in range(1, WGP):
                cols = slice(n * WPC, (n + 1) * WPC)
                pool.wait_ge(w_hi_done, 2 + 2 * n)
                pool.tensor_tensor(wg_lo[:, cols], wg_raw[:, cols], wg_hi[:, cols].bitcast(F32), ALU.subtract)\
                    .then_inc(w_lo_late, 1)
                pool.wait_ge(w_hi_done, 3 + 2 * n)
                pool.tensor_tensor(wu_lo[:, cols], wu_raw[:, cols], wu_hi[:, cols].bitcast(F32), ALU.subtract)\
                    .then_inc(w_lo_late, 1)

            def normalize(slot, mv, centred_sem, xn_sem, rstd_sem, run, first_run):
                wait(pool, rstd_sem, 1, run, 1)
                pool.tensor_tensor(x_centred[:], X[:, slot], mv[:, :, 0:1].to_broadcast([P, NT, D]), ALU.subtract)\
                    .then_inc(centred_sem, 1)
                wait(pool, centred_sem, 1, run, 1 - first_run)
                pool.tensor_tensor(xn[:], x_centred[:], rstd[:].unsqueeze(2).to_broadcast([P, NT, D]), ALU.mult)\
                    .then_inc(xn_sem, 1)

            def unit(u, attn, next_attn, last):
                if isinstance(u, int) and u == LAG - 1:
                    pool.wait_ge(wd_hi_done, 1)
                    pool.tensor_tensor(wd_lo[:], wd_sb[:], wd_hi[:].bitcast(F32), ALU.subtract).then_inc(wd_lo_done, 1)
                for t, e in schedule(attn):
                    if t == X_NORM[attn] and not last:
                        rstd_of(mv, mv_done, eps_done, rstd_done, u + 1)
                        normalize(u + 1, mv, centred_done, xn_done, rstd_done, u + 1, 1)
                    if not attn and e < NP2:
                        wait(pool, gu_done, NP2, u, e + 1)
                        wait(pool, c_copied, NP2, ALONE[u], e + 1)
                        wait(pool, down_done, CH, u, downs_before(e))
                        pool.tensor_tensor(hid[:, e % HIDS, :], gu[:, e % 2, :], c_sb[:, e % 2, :], ALU.mult)\
                            .then_inc(hid_done, 1)
                    if attn and e is not None:
                        wait(pool, hid_done, CH, u, e + 1)
                        pool.tensor_tensor(hid_hi[:, e % HIDS, :], hid[:, e % HIDS, :],
                                           one[:].to_broadcast([P, SEQ]), ALU.mult).then_inc(hid_hi_done, 1)
                        wait(pool, hid_hi_done, CH, u - LAG, e + 1)
                        pool.tensor_tensor(hid_lo[:, e % HIDS, :], hid[:, e % HIDS, :],
                                           hid_hi[:, e % HIDS, :].bitcast(F32), ALU.subtract).then_inc(hid_lo_done, 1)
                    if t == XA_NORM[attn] and next_attn:
                        rstd_of(amv, amv_done, aeps_done, arstd_done, u - 1)
                        normalize(u - 1, amv, acentred_done, axn_done, arstd_done, u - 1, 0)

            units(pool, unit)

        @block.scalar
        def _(act):
            def next_x(run, bank):
                wait(act, xt_psum, 1, run, 1)
                act.activation(xt_next_hi[:], bank[:], ACT.Copy).then_inc(xt_hi_done, 1)

            def logits_lo(run, bank):
                wait(act, logits_psum, 1, run, 1)
                act.activation(r_logit_lo[:], bank[:, 0:NT * 2 * E].rearrange("p (t h e) -> p t h e", t=NT, h=2)
                               [:, :, 1, :], ACT.Copy).then_inc(logits_lo_done, 1)

            def gate_exp(run):
                wait(act, logits_done, 1, run, 1)
                act.activation(r_exp[:], r_logit[:], ACT.Exp, scale=-1.0).then_inc(gate_exp_done, 1)

            act.wait_ge(route_in, 32)
            act.activation(gk_parts[:, 0], gk_raw[:], ACT.Copy).then_inc(w_hi_done, 1)
            next_x(0, pO)

            def weights_hi(n):
                cols = slice(n * WPC, (n + 1) * WPC)
                act.wait_ge(wg_in, 16)
                act.activation(wg_hi[:, cols], wg_raw[:, cols], ACT.Copy).then_inc(w_hi_done, 1)
                act.wait_ge(wu_in, 16)
                act.activation(wu_hi[:, cols], wu_raw[:, cols], ACT.Copy).then_inc(w_hi_done, 1)

            def constants():
                act.wait_ge(wd_in, 16)
                act.activation(wd_hi[:], wd_sb[:], ACT.Copy).then_inc(wd_hi_done, 1)
                act.wait_ge(attn_w_in, 6 * 16)
                act.activation(ident_bf[:], ident[:], ACT.Copy).then_inc(consts_ready, 1)
                act.activation(mask[:], mask_raw[:], ACT.Copy).then_inc(consts_ready, 1)
                act.mul(wq_scaled[:], wq_raw[:], float(HD) ** -0.5).then_inc(wq_scaled_done, 1)
                act.wait_ge(wq_scaled_done, 1)
                for c in range(4):
                    act.activation(wq_hi[:, c, :].rearrange("p (j r d) -> p j r d", j=4, r=4), q_heads(wq_scaled, c),
                                   ACT.Copy).then_inc(attn_hi_done, 1)
                act.activation(wk_hi[:].rearrange("p (r d) -> p r d", d=HD),
                               wk_raw[:].unsqueeze(1).to_broadcast([P, P // HD, HD]), ACT.Copy).then_inc(attn_hi_done, 1)
                act.activation(wv_parts[:, 0], wv_raw[:], ACT.Copy).then_inc(attn_hi_done, 1)

            def move_x_hi(run):
                wait(act, xt_hi_done, 1, run, 1)
                wait(act, u_psum, CH, run, 0)
                act.activation(xt_hi[:], xt_next_hi[:].bitcast(F32), ACT.Copy).then_inc(xt_moved_hi, 1)

            weights_hi(0)
            move_x_hi(0)
            logits_lo(0, pO)
            gate_exp(0)
            weights_hi(1)
            weights_hi(2)

            def unit(u, attn, next_attn, last):
                a = u - LAG
                first = isinstance(u, int) and u == 0
                prep = prep_bank(attn)

                def tanh(e):
                    wait(act, g_psum, CH, u, e + 1)
                    wait(act, sg_done, CH, u, e - 1)
                    act.activation(th[:, e % 2], g_bank(attn, e)[:], ACT.Tanh, scale=0.5).then_inc(tanh_done, 1)

                def qk_high(n):
                    wait(act, qk_psum, 5, a, n + 1)
                    wait(act, qk_done, 5, a, max(n - 1, 0))
                    act.activation(qk_hi[:, n % 2, :], qk_banks[n][:], ACT.Copy).then_inc(qk_hi_done, 1)

                def copy_probs(i, h):
                    wait(act, t_psum, 2 * NBLK, a, 2 * i + h + 1)
                    wait(act, o_psum, NBLK, a, i - 1)
                    act.activation(prob_t[:, i % 2, 4 * h:4 * h + 4, :], pT[:].rearrange("p (s k) -> p s k", s=4),
                                   ACT.Copy).then_inc(t_copied, 1)

                def exps(i, h):
                    wait(act, max_done, 2 * NBLK, a, 2 * i + h + 1)
                    wait(act, t_psum, 2 * NBLK, a, 2 * i + h - 3)
                    for s in range(4 * h, 4 * h + 4):
                        ins = act.activation(prob[:, i % 2, s, :], (pS0, pS1)[h][:, P * (s % 4):P * (s % 4 + 1)],
                                             ACT.Exp, bias=neg_max[:, s:s + 1])
                    ins.then_inc(exp_done, 1)

                def combine_columns():
                    wait(act, comb_psum, 1, u, 1)
                    act.activation(comb_t[:], prep[:], ACT.Copy).then_inc(comb_t_done, 1)

                def copy_y():
                    wait(act, down_done, CH, u, 0)
                    act.activation(y_sb[:], pY[:], ACT.Copy).then_inc(y_copied, 1)

                def output_columns(b, i):
                    wait(act, ot_psum, NBLK, b, i + 1)
                    act.activation(o_t[0:P // 2, :, QB * i:QB * (i + 1)],
                                   pG[0:P // 2, 0:P].rearrange("p (c q) -> p c q", c=2),
                                   ACT.Copy).then_inc(ot_copied, 1)

                for t, e in schedule(attn):
                    if attn and t == 0:
                        if isinstance(u, int):
                            act.wait_ge(zeroed, 10)
                        for n in range(3):
                            qk_high(n)
                    if t == 0 and later_attention(u):
                        output_columns(a - 1, NBLK - 1)
                    if attn and t == 0:
                        qk_high(3)
                    if e is not None and (attn or e == 0):
                        tanh(e)
                    if e == 0 and not first:
                        combine_columns()
                    if not attn and e + 1 < CH:
                        tanh(e + 1)
                    if not attn and e == CH - 1 and not last:
                        move_x_hi(u + 1)
                    if first and e == 0:
                        act.wait_ge(const_in, 32)
                        act.activation(sel[:], sel_raw[:], ACT.Copy).then_inc(consts_ready, 1)
                    if first and e == 0:
                        combine_columns()
                    if t == X_COLUMNS[attn] and not last:
                        next_x(u + 1, prep)
                    if t == XA_COLUMNS[attn] and next_attn:
                        wait(act, xa_psum, 1, u - 1, 1)
                        act.activation(xa_hi[:], prep[:], ACT.Copy).then_inc(xa_hi_done, 1)
                    if not attn and e < NP2:
                        wait(act, c_psum, NP2, u, e + 1)
                        wait(act, hid_done, CH, u, e - 1)
                        act.activation(c_sb[:, e % 2, :], c_bank(attn, e)[:], ACT.Copy).then_inc(c_copied, 1)
                    if first and e == 4:
                        constants()
                    if attn and t == 0:
                        qk_high(4)
                        for j in (0, 1):
                            rows = slice(32 * j, 32 * j + 32)
                            wait(act, qk_done, 5, a, 4)
                            act.activation(k_diag[rows, j, :], k_all[rows, :].bitcast(F32), ACT.Copy)\
                                .then_inc(k_diag_done, 1)
                        wait(act, v_psum, 1, a, 1)
                        act.activation(v_lo[:], v_bank[:, 0:NBLK * 2 * HD]
                                       .rearrange("p (i h d) -> p i h d", h=2, d=HD)[:, :, 1, :],
                                       ACT.Copy).then_inc(v_lo_done, 1)
                    if attn and 2 <= t < NBLK + 2:
                        copy_probs(t - 2, 0)
                    if attn and 1 <= t < NBLK + 1:
                        exps(t - 1, 0)
                    if attn and 3 <= t < NBLK + 3:
                        wait(act, o_psum, NBLK, a, t - 2)
                        act.activation(o_raw[:], pO[:, 0:BACK], ACT.Copy).then_inc(o_copied, 1)
                    if attn and 4 <= t < NBLK + 3:
                        output_columns(a, t - 4)
                    if attn and e == CH - 1:
                        move_x_hi(u + 1)
                    if attn and t == 2:
                        copy_probs(0, 1)
                    if attn and 1 <= t < NBLK + 1:
                        exps(t - 1, 1)
                    if t == LOGITS[attn] and not last:
                        logits_lo(u + 1, prep)
                    if attn and 3 <= t < NBLK + 2:
                        copy_probs(t - 2, 1)
                    if t == LOGITS[attn] and not last:
                        gate_exp(u + 1)
                    if t == Y_DONE[attn] and not first:
                        copy_y()

            units(act, unit)
            act.wait_ge(down_done, CH * UNITS)
            act.activation(y_sb[:], pY[:], ACT.Copy).then_inc(y_copied, 1)

        @block.vector
        def _(dve):
            def wait_by_memset(s, per, index, k):
                wait(dve, s, per, index, k)
                if not isinstance(index, int):
                    dve.memset(pause[:], 0.0)

            def layernorm(slot, sems, run):
                s_stats, s_mv, to = sems
                for t in range(NT):
                    dve.bn_stats(stats[:, t, :], X[:, slot, t, :]).then_inc(s_stats, 1)
                wait_by_memset(s_stats, NT, run, NT)
                for t in range(NT):
                    dve.bn_aggr(to[:, t, :], stats[:, t, :]).then_inc(s_mv, 1)

            F_LN = (stats_done, mv_done, mv)
            A_LN = (astats_done, amv_done, amv)

            def route(run, k):
                if k == 1:
                    wait(dve, gate_exp_done, 1, run, 1)
                elif k == 14:
                    wait_by_memset(route_step, ROUTE_STEPS, run, k - 1)
                else:
                    need = {5: 3, 6: 3, 9: 7, 16: 14, 17: 15}.get(k, k - 1)
                    wait(dve, route_step, ROUTE_STEPS, run, need)
                choice = r_choice[:].rearrange("p t (g i) -> p (t g) i", g=GROUPS)
                other = r_group[:].unsqueeze(2).to_broadcast([P, NT, GROUPS, GROUPS])
                own = r_group[:].unsqueeze(3).to_broadcast([P, NT, GROUPS, GROUPS])
                fourth = r_top8[:, :, TOP_K - 1:TOP_K].to_broadcast([P, NT, E])
                if k == 1:
                    ins = dve.tensor_scalar(r_den[:], r_exp[:], 1.0, None, ALU.add)
                elif k == 2:
                    ins = dve.reciprocal(r_score[:], r_den[:])
                elif k == 3:
                    ins = dve.tensor_tensor(r_choice[:], r_score[:],
                                            gbias_sb[:].unsqueeze(1).to_broadcast([P, NT, E]), ALU.add)
                elif k == 4:
                    ins = dve.tensor_tensor(r_pair[:, :, 0:3], choice[:, :, 0:3], choice[:, :, 1:4], ALU.add)
                elif k == 5:
                    ins = dve.tensor_tensor(r_pair[:, :, 3:5], choice[:, :, 0:2], choice[:, :, 2:4], ALU.add)
                elif k == 6:
                    ins = dve.tensor_tensor(r_pair[:, :, 5:6], choice[:, :, 0:1], choice[:, :, 3:4], ALU.add)
                elif k == 7:
                    ins = dve.tensor_reduce(r_group[:].rearrange("p t g -> p (t g)"), r_pair[:], AX.X, ALU.max)
                elif k == 8:
                    ins = dve.tensor_tensor(r_gt[:], other, own, ALU.is_gt)
                elif k == 9:
                    ins = dve.tensor_tensor(r_eq[:], other, own, ALU.is_equal)
                elif k == 10:
                    ins = dve.tensor_tensor(r_eq_tri[:], r_eq[:],
                                            tri[:].unsqueeze(1).to_broadcast([P, NT, GROUPS, GROUPS]), ALU.mult)
                elif k == 11:
                    ins = dve.tensor_tensor(r_before[:], r_gt[:], r_eq_tri[:], ALU.add)
                elif k == 12:
                    ins = dve.tensor_reduce(r_rank[:], r_before[:].rearrange("p t g j -> p (t g) j"), AX.X, ALU.add)
                elif k == 13:
                    ins = dve.scalar_tensor_tensor(r_masked[:].rearrange("p t (g i) -> p (t g) i", g=GROUPS),
                                                   r_rank[:].unsqueeze(2)
                                                   .to_broadcast([P, NT * GROUPS, E // GROUPS]),
                                                   float(TOP_GROUPS), choice, ALU.is_lt, ALU.mult)
                elif k == 14:
                    for t in range(NT):
                        ins = dve.max(r_top8[:, t, :], r_masked[:, t, :])
                elif k == 15:
                    ins = dve.tensor_tensor(r_above[:], r_masked[:], fourth, ALU.is_gt)
                elif k == 16:
                    ins = dve.tensor_tensor(r_tie[:, :, 1:], r_masked[:], fourth, ALU.is_equal)
                elif k == 17:
                    ins = dve.tensor_reduce(r_tie[:, :, 0], r_above[:], AX.X, ALU.add)
                elif k == 18:
                    ins = dve.tensor_tensor_scan(r_count[:].rearrange("p t e -> p (t e)"),
                                                 r_carry[:].rearrange("p t e -> p (t e)"),
                                                 r_tie[:].rearrange("p t e -> p (t e)"), 0.0, ALU.mult, ALU.add)
                elif k == 19:
                    ins = dve.scalar_tensor_tensor(r_tie_in[:], r_count[:, :, 1:], float(TOP_K), r_tie[:, :, 1:],
                                                   ALU.is_le, ALU.mult)
                elif k == 20:
                    ins = dve.tensor_tensor(r_pick[:], r_tie_in[:], r_above[:], ALU.add)
                elif k == 21:
                    ins = dve.tensor_tensor(r_w[:], r_pick[:], r_masked[:], ALU.mult)
                elif k == 22:
                    ins = dve.tensor_reduce(r_sum[:], r_w[:], AX.X, ALU.add)
                elif k == 23:
                    ins = dve.tensor_scalar(r_sum_eps[:], r_sum[:], 1e-20, None, ALU.add)
                elif k == 24:
                    ins = dve.reciprocal(r_inv[:], r_sum_eps[:])
                elif k == 25:
                    ins = dve.scalar_tensor_tensor(r_comb[:], r_w[:], ROUTE_SCALE, r_inv[:].unsqueeze(2)
                                                   .to_broadcast([P, NT, E]), ALU.mult, ALU.mult)
                elif k == 26:
                    wait(dve, comb_psum, 1, run, 0)
                    ins = dve.tensor_copy(comb[:, :, 0:E].bitcast(F32R), r_comb[:])
                elif k == 27:
                    ins = dve.tensor_tensor(comb[:, :, E:2 * E].bitcast(F32R), r_comb[:], comb[:, :, 0:E],
                                            ALU.subtract)
                ins.then_inc(route_step, 1)

            def route_part(run, attn, t, m):
                parts = [(tick, n, count) for tick, counts in (ROUTE_ATTN if attn else ROUTE_ALONE).items()
                         for n, count in enumerate(counts)]
                done = sum(count for tick, n, count in parts if (tick, n) < (t, m))
                here = sum(count for tick, n, count in parts if (tick, n) == (t, m))
                for k in range(done + 1, done + here + 1):
                    route(run, k)

            def next_x_lo(run, bank):
                wait(dve, xt_hi_done, 1, run, 1)
                dve.tensor_tensor(xt_next_lo[:], bank[:], xt_next_hi[:].bitcast(F32), ALU.subtract)\
                   .then_inc(xt_lo_done, 1)

            dve.wait_ge(x_in[0], 16)
            layernorm(0, F_LN, 0)
            dve.wait_ge(w_hi_done, 1)
            dve.tensor_tensor(gk_parts[:, 1], gk_raw[:], gk_parts[:, 0].bitcast(F32), ALU.subtract).then_inc(w_lo_done, 1)
            dve.wait_ge(mv_done, NT)
            dve.wait_ge(rstd_done, 1)
            for t in range(NT):
                ins = dve.tensor_scalar(xn[:, t, :], X[:, 0, t, :], mv[:, t, 0:1], rstd[:, t:t + 1],
                                        ALU.subtract, ALU.mult)
            ins.then_inc(xn_done, 1)
            next_x_lo(0, pO)

            def sum_logits(run, bank):
                wait(dve, logits_lo_done, 1, run, 1)
                dve.tensor_tensor(r_logit[:], bank[:, 0:NT * 2 * E].rearrange("p (t h e) -> p t h e", t=NT, h=2)
                                  [:, :, 0, :], r_logit_lo[:], ALU.add).then_inc(logits_done, 1)

            def move_x_lo(run):
                wait(dve, xt_lo_done, 1, run, 1)
                wait(dve, u_psum, CH, run, 0)
                dve.tensor_copy(xt_lo[:], xt_next_lo[:].bitcast(F32)).then_inc(xt_moved_lo, 1)

            cols = slice(0, WPC)
            dve.wait_ge(w_hi_done, 2)
            dve.tensor_tensor(wg_lo[:, cols], wg_raw[:, cols], wg_hi[:, cols].bitcast(F32), ALU.subtract)\
               .then_inc(w_lo_done, 1)
            dve.wait_ge(w_hi_done, 3)
            dve.tensor_tensor(wu_lo[:, cols], wu_raw[:, cols], wu_hi[:, cols].bitcast(F32), ALU.subtract)\
               .then_inc(w_lo_done, 1)
            move_x_lo(0)
            sum_logits(0, pO)

            def unit(u, attn, next_attn, last):
                a = u - LAG
                if isinstance(u, int) and u == 1:
                    dve.wait_ge(zeroed, 10)
                def attention_weights_lo():
                    for c in range(4):
                        dve.wait_ge(attn_hi_done, c + 1)
                        dve.tensor_tensor(wq_lo[:, c, :].rearrange("p (j r d) -> p j r d", j=4, r=4),
                                          q_heads(wq_scaled, c),
                                          wq_hi[:, c, :].bitcast(F32).rearrange("p (j r d) -> p j r d", j=4, r=4),
                                          ALU.subtract).then_inc(attn_lo_done, 1)
                    dve.wait_ge(attn_hi_done, 6)
                    dve.tensor_tensor(wk_lo[:].rearrange("p (r d) -> p r d", d=HD),
                                      wk_raw[:].unsqueeze(1).to_broadcast([P, P // HD, HD]),
                                      wk_hi[:].bitcast(F32).rearrange("p (r d) -> p r d", d=HD), ALU.subtract)\
                       .then_inc(attn_lo_done, 1)
                    dve.tensor_tensor(wv_parts[:, 1], wv_raw[:], wv_parts[:, 0].bitcast(F32), ALU.subtract)\
                       .then_inc(attn_lo_done, 1)

                def q_part(c):
                    n = c if c < 3 else 4
                    wait(dve, qk_hi_done, 5, a, n + 1)
                    dve.scalar_tensor_tensor(q_rep[:, c // 2, :, c % 2, :],
                                             qk_hi[:, n % 2, :].bitcast(F32).rearrange("p (i q) -> p i q", q=QB),
                                             beta[:, 0:1], qk_banks[n][:].rearrange("p (i q) -> p i q", q=QB),
                                             ALU.mult, ALU.add).then_inc(qk_done, 1)

                def k_part():
                    wait(dve, qk_hi_done, 5, a, 4)
                    dve.scalar_tensor_tensor(k_all[:], qk_hi[:, 1, :].bitcast(F32), beta[:, 1:2], k_bank[:],
                                             ALU.mult, ALU.add).then_inc(qk_done, 1)
                    for j in (2, 3):
                        rows = slice(32 * j, 32 * j + 32)
                        wait(dve, qk_done, 5, a, 4)
                        dve.tensor_copy(k_diag[rows, j, :], k_all[rows, :].bitcast(F32)).then_inc(k_diag_done, 1)

                def chunk_gate(e):
                    wait(dve, tanh_done, CH, u, e + 1)
                    dve.scalar_tensor_tensor(sg[:, e % 2, :], th[:, e % 2], 1.0, g_bank(attn, e)[:], ALU.add, ALU.mult)\
                       .then_inc(sg_done, 1)

                def chunk_up(e):
                    wait(dve, sg_done, CH, u, e + 1)
                    wait(dve, u_psum, CH, u, e + 1)
                    up = u_bank(attn, e)
                    if e == CH - 1:
                        if not attn:
                            wait(dve, hid_done, CH, u, e)
                        wait(dve, down_done, CH, u, downs_before(e))
                        dve.scalar_tensor_tensor(hid[:, e % HIDS, :], sg[:, e % 2, :], 0.5, up[:], ALU.mult, ALU.mult)\
                           .then_inc(hid_done, 1)
                    else:
                        wait(dve, hid_done, CH, u, e - 1)
                        dve.scalar_tensor_tensor(gu[:, e % 2, :], sg[:, e % 2, :], 0.5, up[:], ALU.mult, ALU.mult)\
                           .then_inc(gu_done, 1)

                def chunk_weight(e):
                    wait(dve, gu_done, NP2, u, e + 1)
                    wait(dve, c_psum, NP2, u, e + 1)
                    wait(dve, down_done, CH, u, downs_before(e))
                    dve.tensor_tensor(hid[:, e % HIDS, :], gu[:, e % 2, :], c_bank(attn, e)[:], ALU.mult)\
                       .then_inc(hid_done, 1)

                def negated_max(i, h):
                    wait(dve, s_psum, 2 * NBLK, a, 2 * i + h + 1)
                    wait(dve, exp_done, 2 * NBLK, a, 2 * i + h - 1)
                    dve.tensor_reduce(neg_max[:, 4 * h:4 * h + 4], (pS0, pS1)[h][:].rearrange("p (s k) -> p s k", s=4),
                                      AX.X, ALU.max, negate=True).then_inc(max_done, 1)

                def add_output():
                    wait(dve, y_back, 1, u, 0)
                    dve.scalar_tensor_tensor(X[:, u - 1].rearrange("p t d -> p (t d)"), pO[:], 0.5,
                                             X[:, u - 1].rearrange("p t d -> p (t d)"), ALU.mult, ALU.add)\
                       .then_inc(x_added, 1)

                def next_layernorm():
                    if isinstance(u, int) and u + 1 < NB:
                        dve.wait_ge(x_in[u + 1], 16)
                    else:
                        wait_apart(dve, attn_added, 1, u, 2 - NB)
                    layernorm(u + 1, F_LN, u + 1)

                first = isinstance(u, int) and u == 0
                prep = prep_bank(attn)
                for t, e in schedule(attn):
                    if attn and t == 0:
                        if isinstance(u, int):
                            dve.wait_ge(zeroed, 10)
                        q_part(0)
                        q_part(1)
                        q_part(2)
                        k_part()
                    if attn and 1 <= t < NBLK + 1:
                        negated_max(t - 1, 0)
                    if attn and t == X_ADD[attn]:
                        add_output()
                    if e == 0 and later_attention(u):
                        wait(dve, attn_psum, 1, a, 0)
                        dve.tensor_tensor(X[:, u - 1 - LAG + NB].rearrange("p t d -> p (t d)"), pS0[:],
                                          X[:, u - 1 - LAG].rearrange("p t d -> p (t d)"), ALU.add)\
                           .then_inc(attn_added, 1)
                    if attn and t == X_NORM[attn]:
                        next_layernorm()
                    if first and e == 0:
                        dve.wait_ge(zeroed, 6)
                        dve.wait_ge(const_in, 32)
                        dve.wait_ge(route_in, 32)
                        for k in range(1, ROUTE_STEPS + 1):
                            route(0, k)
                    if t == X_NORM[attn] and not (attn or first or last):
                        next_layernorm()
                    if e is not None:
                        chunk_gate(e)
                    if attn and t == 1:
                        negated_max(0, 1)
                    if e == CH - 1 and not last:
                        move_x_lo(u + 1)
                    if not last:
                        route_part(u + 1, attn, t, 0)
                    if e is not None:
                        chunk_up(e)
                    if t == X_COLUMNS[attn] and not last:
                        next_x_lo(u + 1, prep)
                    if t == XA_COLUMNS[attn] and next_attn:
                        wait(dve, xa_hi_done, 1, u - 1, 1)
                        dve.tensor_tensor(xa_lo[:], prep[:], xa_hi[:].bitcast(F32), ALU.subtract)\
                           .then_inc(xa_lo_done, 1)
                    if attn and 2 <= t < NBLK + 1:
                        negated_max(t - 1, 1)
                    if not last:
                        route_part(u + 1, attn, t, 1)
                    if attn and t == 0:
                        q_part(3)
                        wait(dve, v_lo_done, 1, a, 1)
                        wait(dve, o_psum, NBLK, a, 0)
                        dve.tensor_tensor(v_one[:, :, 0:HD], v_bank[:, 0:NBLK * 2 * HD]
                                          .rearrange("p (i h d) -> p i h d", h=2, d=HD)[:, :, 0, :], v_lo[:],
                                          ALU.add).then_inc(v_done, 1)
                    if attn and e is not None and e < NP2:
                        chunk_weight(e)
                    if not attn and t == X_ADD[attn] and not first:
                        add_output()
                    o_all = pO[:, BACK:2 * BACK].rearrange("p (s r) -> p s r", r=32)
                    if attn and 3 <= t < NBLK + 3:
                        wait(dve, back_psum, NBLK, a, t - 2)
                        dve.reciprocal(o_inv[:], o_all[:, :, HD]).then_inc(o_inv_done, 1)
                    if not last:
                        route_part(u + 1, attn, t, 2)
                    if attn and 3 <= t < NBLK + 3:
                        wait(dve, o_inv_done, NBLK, a, t - 2)
                        wait(dve, ot_psum, NBLK, a, t - 3)
                        dve.tensor_tensor(o_norm[:], o_all[:, :, 0:HD], o_inv[:].unsqueeze(2)
                                          .to_broadcast([P, 8, HD]), ALU.mult).then_inc(o_norm_done, 1)
                    if t == LOGITS[attn] and not last:
                        sum_logits(u + 1, prep)
                    if isinstance(u, int) and u == 1 and e == 2:
                        attention_weights_lo()
                    if t == X_NORM[attn] and first:
                        next_layernorm()
                    if t == XA_NORM[attn] and next_attn:
                        wait_apart(dve, x_added, 1, u, 0)
                        layernorm(u - 1, A_LN, u - 1)

            units(dve, unit)
            dve.wait_ge(y_back, UNITS)
            dve.scalar_tensor_tensor(X[:, UNITS - 1].rearrange("p t d -> p (t d)"), pO[:], 0.5,
                                     X[:, UNITS - 1].rearrange("p t d -> p (t d)"), ALU.mult, ALU.add)\
               .then_inc(x_added, 1)

        @block.tensor
        def _(pe):
            def three(dst, w_hi, w_lo, x_hi, x_lo, start=True):
                pe.matmul(dst, w_hi, x_hi, start=start, stop=False)
                pe.matmul(dst, w_lo, x_hi, start=False, stop=False)
                return pe.matmul(dst, w_hi, x_lo, start=False, stop=True)

            def to_columns(bank, done, xn_sem, run):
                wait(pe, xn_sem, 1, run, 1)
                for t in range(NT):
                    ins = pe.transpose(bank[:, P * t:P * (t + 1)], xn[:, t, :], ident[:])
                ins.then_inc(done, 1)

            def logits(run, bank):
                wait(pe, xt_hi_done, 1, run, 1)
                wait(pe, xt_lo_done, 1, run, 1)
                for t in range(NT):
                    tok = slice(P * t, P * (t + 1))
                    dst = bank[:, 2 * E * t:2 * E * (t + 1)]
                    parts = gk_parts[:].rearrange("p h e -> p (h e)")
                    pe.matmul(dst, xt_next_hi[:, tok], parts, start=True, stop=False)
                    ins = pe.matmul(dst, xt_next_lo[:, tok], parts, start=False, stop=True)
                ins.then_inc(logits_psum, 1)

            def down(n, e, split, first_unit=False):
                if split:
                    wait(pe, hid_lo_done, CH, n - LAG, e + 1)
                else:
                    wait(pe, hid_done, CH, n, e + 1)
                if e == 0:
                    wait(pe, y_copied, 1, n, 0)
                if first_unit and e == 0:
                    pe.wait_ge(wd_in, 16)
                start, stop = e == 0, e == CH - 1
                if split:
                    pe.matmul(pY[:], wd_hi[:, e, :], hid_hi[:, e % HIDS, :], start=start, stop=False)
                    pe.matmul(pY[:], wd_lo[:, e, :], hid_hi[:, e % HIDS, :], start=False, stop=False)
                    pe.matmul(pY[:], wd_hi[:, e, :], hid_lo[:, e % HIDS, :], start=False, stop=stop)\
                      .then_inc(down_done, 1)
                else:
                    pe.matmul(pY[:], wd_sb[:, e, :], hid[:, e % HIDS, :], start=start, stop=stop).then_inc(down_done, 1)

            def y_to_rows(n, bank):
                wait(pe, y_copied, 1, n, 1)
                wait(pe, x_added, 1, n, 0)
                for s in range(NT):
                    ins = pe.transpose(bank[:, P * s:P * (s + 1)], y_sb[:, P * s:P * (s + 1)], ident[:])
                ins.then_inc(y_back, 1)

            pe.wait_ge(zeroed, 6)
            for _ in range(3):
                pe.matmul(pY[:], comb[:, 0, :], comb[:].rearrange("p t k -> p (t k)"), start=True, stop=True)
            pe.wait_ge(ident_loaded, 16)
            to_columns(pO, xt_psum, xn_done, 0)
            pe.wait_ge(w_hi_done, 1)
            pe.wait_ge(w_lo_done, 1)
            logits(0, pO)

            def unit(u, attn, next_attn, last):
                a = u - LAG
                first = isinstance(u, int) and u == 0
                prep = prep_bank(attn)

                def gate(t, e):
                    if attn and t >= 5:
                        wait(pe, ot_copied, NBLK, a, t - 4)
                    if e == 0:
                        wait(pe, xt_moved_hi, 1, u, 1)
                        wait(pe, xt_moved_lo, 1, u, 1)
                        wait(pe, sg_done, CH, u, 0)
                        wait(pe, hid_done, CH, u, 0)
                    if first:
                        n = (P * (e + 1) - 1) // WPC
                        pe.wait_ge(*((w_lo_late, 2 * n) if n else (w_lo_done, 3)))
                    if e == 1 and isinstance(u, int) and u == LAG + NB:
                        pe.wait_ge(attn_added, NB)
                    cols = slice(P * e, P * (e + 1))
                    before = e if attn else e - 1
                    if e > 0:
                        wait(pe, sg_done, CH, u, before)
                    three(g_bank(attn, e)[:], wg_hi[:, cols], wg_lo[:, cols], xt_hi[:], xt_lo[:]).then_inc(g_psum, 1)

                def up(e):
                    cols = slice(P * e, P * (e + 1))
                    if e > 0:
                        wait(pe, gu_done, NP2, u, e if attn else e - 1)
                    three(u_bank(attn, e)[:], wu_hi[:, cols], wu_lo[:, cols], xt_hi[:], xt_lo[:]).then_inc(u_psum, 1)

                def combine(e):
                    if e == 0:
                        wait(pe, comb_t_done, 1, u, 1)
                        if first:
                            pe.wait_ge(consts_ready, 1)
                    elif attn:
                        wait(pe, hid_done, CH, u, e)
                        if e == CHUNK_TICKS.index(LOGITS[attn] + 1):
                            wait(pe, logits_done, 1, u + 1, 1)
                        if e == CHUNK_TICKS.index(XA_COLUMNS[attn] + 1) and next_attn:
                            wait(pe, xa_lo_done, 1, u - 1, 1)
                    else:
                        wait(pe, c_copied, NP2, ALONE[u], e - 1)
                    pe.matmul(c_bank(attn, e)[:], sel[:, e, :], comb_t[:], start=True, stop=True).then_inc(c_psum, 1)

                def combine_to_columns():
                    wait(pe, route_step, ROUTE_STEPS, u, ROUTE_STEPS)
                    if attn:
                        wait(pe, hid_done, CH, u, -1)
                    for s in range(NT):
                        ins = pe.transpose(prep[:, P * s:P * (s + 1)], comb[:, s, :], ident[:])
                    ins.then_inc(comb_psum, 1)

                def columns(t):
                    if t == X_COLUMNS[attn] and not last:
                        if attn:
                            wait(pe, hid_done, CH, u, t)
                        else:
                            wait(pe, comb_t_done, 1, u, 1)
                            wait(pe, x_added, 1, u, 0)
                        to_columns(prep, xt_psum, xn_done, u + 1)
                    if t == XA_COLUMNS[attn] and next_attn:
                        if attn:
                            wait(pe, hid_done, CH, u, t - 1)
                        wait(pe, logits_done, 1, u + 1, 1)
                        to_columns(prep, xa_psum, axn_done, u - 1)

                def transpose_probs(i, h):
                    wait(pe, exp_done, 2 * NBLK, a, 2 * i + h + 1)
                    wait(pe, t_copied, 2 * NBLK, a, 2 * i + h)
                    if i == 0 and h == 0:
                        wait(pe, v_done, 1, a, 1)
                    for s in range(4):
                        ins = pe.transpose(pT[:, P * s:P * (s + 1)], prob[:, i % 2, 4 * h + s, :], ident[:])
                    ins.then_inc(t_psum, 1)

                def weighted_values(i):
                    wait(pe, t_copied, 2 * NBLK, a, 2 * i + 2)
                    wait(pe, o_norm_done, NBLK, a, i)
                    if i == 0:
                        wait(pe, x_added, 1, u, 0)
                    for j in range(4):
                        ins = pe.matmul(pO[32 * j:32 * j + 32, 0:BACK], v_one[:, i, :],
                                        prob_t[:, i % 2].rearrange("p (h j) q -> p j h q", h=2)[:, j, :, :],
                                        start=True, stop=True)
                    ins.then_inc(o_psum, 1)

                def gate_bank_free(b, i, gates):
                    wait(pe, sg_done, CH, u, gates)
                    wait(pe, ot_copied, NBLK, b, i)

                def output_to_rows(i):
                    wait(pe, o_copied, NBLK, a, i + 1)
                    for h in range(2):
                        ins = pe.transpose(pO[:, BACK + P * h:BACK + P * (h + 1)], o_raw[:, P * h:P * (h + 1)],
                                           ident[:])
                    ins.then_inc(back_psum, 1)

                def output_to_columns(b, i):
                    wait_apart(pe, o_norm_done, NBLK, b, i + 1)
                    pe.transpose(pG[0:P // 2, 0:P], o_norm[:].rearrange("p s d -> p (s d)"), ident[:])\
                      .then_inc(ot_psum, 1)

                def scores(i, h):
                    if i == 0 and h == 0:
                        wait(pe, qk_done, 5, a, 5)
                        wait(pe, k_diag_done, 4, a, 4)
                    ks = key_start(i)
                    bank = (pS0, pS1)[h]
                    wait(pe, exp_done, 2 * NBLK, a, 2 * i + h - 1)
                    pe.matmul(bank[:], ident_bf[:], mask[:, mask_kind(i):mask_kind(i) + 1, :]
                              .to_broadcast([P, 4, P]), start=True, stop=False)
                    pe.matmul(bank[:], q_rep[:, h, i, :, :].rearrange("p c q -> p (c q)"),
                              k_diag[:, :, ks:ks + P], start=False, stop=True).then_inc(s_psum, 1)

                def project():
                    wait(pe, ot_copied, NBLK, a, 0)
                    wait(pe, exp_done, 2 * NBLK, a, 0)
                    for s in range(NT):
                        tok = slice(P * s, P * (s + 1))
                        dst = pS0[:, P * s:P * (s + 1)]
                        pe.matmul(dst, o_t[:, 0, tok], wf_sb[:, 0, :], start=True, stop=False)
                        ins = pe.matmul(dst, o_t[:, 1, tok], wf_sb[:, 1, :], start=False, stop=True)
                    ins.then_inc(attn_psum, 1)

                for t, e in schedule(attn):
                    if attn and t == 0:
                        if isinstance(u, int):
                            pe.wait_ge(attn_lo_done, 6)
                            pe.wait_ge(consts_ready, 3)
                            pe.wait_ge(wd_lo_done, 1)
                            pe.wait_ge(zeroed, 10)
                            pe.wait_ge(gu_done, NP2 * u)
                            pe.wait_ge(c_copied, NP2 * LAG)
                        wait(pe, xa_hi_done, 1, a, 1)
                        wait(pe, xa_lo_done, 1, a, 1)
                        wait(pe, exp_done, 2 * NBLK, a, 0)
                        wait(pe, t_copied, 2 * NBLK, a, 0)
                        for c in range(3):
                            if c == 2:
                                wait(pe, o_norm_done, NBLK, a, 0)
                                gate_bank_free(a, -1, 0)
                            three(qk_banks[c][:], wq_hi[:, c, :], wq_lo[:, c, :], xa_hi[:], xa_lo[:])\
                                .then_inc(qk_psum, 1)
                    if t == 0 and later_attention(u):
                        if not attn:
                            gate_bank_free(a, -1, 0)
                        output_to_columns(a, -1)
                    if attn and t == 0:
                        wait(pe, qk_done, 5, a, 1)
                        three(k_bank[:], wk_hi[:], wk_lo[:], xa_hi[:], xa_lo[:]).then_inc(qk_psum, 1)
                    if e == 0 and not first:
                        down(u - 1, CH - 2, later_attention(u))
                    if t == 0 and later_attention(u):
                        project()
                    if e is not None and (attn or e == 0):
                        gate(t, e)
                    if attn and 1 <= t < NBLK + 1:
                        scores(t - 1, 0)
                    if attn:
                        columns(t)
                    if attn and 2 <= t < NBLK + 2:
                        transpose_probs(t - 2, 0)
                    if attn and t == NBLK + 2:
                        weighted_values(t - 3)
                    if e is not None and (attn or e == 0):
                        up(e)
                    if e == 0 and not first:
                        combine_to_columns()
                    if not attn and e + 1 < CH:
                        gate(t, e + 1)
                        up(e + 1)
                    if not attn:
                        columns(t)
                    if first and e == 0:
                        for _ in range(3):
                            pe.matmul(pY[:], wg_raw[:, 0:P], wg_raw[:, 0:SEQ], start=True, stop=True)
                        combine_to_columns()
                    if attn and 1 <= t < NBLK + 1:
                        scores(t - 1, 1)
                    if attn and 4 <= t < NBLK + 2:
                        gate_bank_free(a, t - 4, e + 1 if e is not None else CHUNK_TICKS.index(t - 1) + 1)
                    if attn and 3 <= t < NBLK + 2:
                        weighted_values(t - 3)
                    if attn and t == 0:
                        wait(pe, attn_added, 1, a, 0)
                        three(qk_banks[4][:], wq_hi[:, 3, :], wq_lo[:, 3, :], xa_hi[:], xa_lo[:])\
                            .then_inc(qk_psum, 1)
                        wait(pe, qk_done, 5, a, 2)
                        for i in range(NBLK):
                            keys = slice(key_start(i), key_start(i) + P)
                            dst = v_bank[:, 2 * HD * i:2 * HD * (i + 1)]
                            parts = wv_parts[:].rearrange("p h d -> p (h d)")
                            pe.matmul(dst, xa_hi[:, keys], parts, start=True, stop=False)
                            ins = pe.matmul(dst, xa_lo[:, keys], parts, start=False, stop=True)
                        ins.then_inc(v_psum, 1)
                    if t == Y_ROWS[attn] and not first:
                        if not attn:
                            wait(pe, comb_t_done, 1, u, 1)
                        y_to_rows(u - 1, pO)
                    if e is not None and e < NP2:
                        combine(e)
                    if attn and 4 <= t < NBLK + 2:
                        output_to_columns(a, t - 4)
                    if t == Y_DONE[attn] and not first:
                        down(u - 1, CH - 1, later_attention(u))
                    if t in DOWNS[attn]:
                        down(u, DOWNS[attn][t], attn, first)
                    if attn and 3 <= t < NBLK + 3:
                        if t == NBLK + 2:
                            gate_bank_free(a, t - 4, CH)
                        output_to_rows(t - 3)
                    if attn and t == NBLK + 2:
                        output_to_columns(a, t - 4)
                    if t == LOGITS[attn] and not last:
                        logits(u + 1, prep)
                    if attn and 2 <= t < NBLK + 2:
                        transpose_probs(t - 2, 1)

            units(pe, unit)
            down(UNITS - 1, CH - 2, False)
            down(UNITS - 1, CH - 1, False)
            y_to_rows(UNITS - 1, pO)


def kernel(**inputs):
    import numpy as np
    import concourse.bacc as bacc
    from concourse.bass_utils import run_bass_kernel_spmd

    def a(name):
        return np.asarray(inputs[name])

    def put(z):
        return np.ascontiguousarray(z)

    wg = np.concatenate([a("L0_ffn_w_gate").transpose(1, 0, 2).reshape(D, E * M), a("L0_ffn_sw_gate")], 1)
    wu = np.concatenate([a("L0_ffn_w_up").transpose(1, 0, 2).reshape(D, E * M), a("L0_ffn_sw_up")], 1)
    wd = np.concatenate([a("L0_ffn_w_down").reshape(NP2, P, D), a("L0_ffn_sw_down")[None]], 0).transpose(1, 0, 2)
    q = np.arange(P)[:, None] % QB
    k = np.arange(P)[None, :]
    first_key = [0, -WINDOW, -QB]
    mask = np.stack([np.where(np.abs(q - (k + s)) <= WINDOW, 0.0, -1e30) for s in first_key], 1).astype(np.float32)
    sel = np.zeros((P, NP2, P), np.float32)
    for e in range(E):
        sel[[e, E + e], e // 2, (e % 2) * M:(e % 2 + 1) * M] = 1.0
    tri = np.broadcast_to(np.tril(np.ones((GROUPS, GROUPS), np.float32), -1), (P, GROUPS, GROUPS))
    part = np.arange(P) // HD % 4
    beta = np.stack([np.where(part >= 2, -1.0, 0.0), np.where(part % 2 == 1, -1.0, 0.0)], 1).astype(np.float32)
    arrays = {
        "x": put(a("L0_attn_x").reshape(NB * SEQ, D)), "wg": put(wg), "wu": put(wu), "wd": put(wd),
        "gk": put(a("L0_ffn_gate_kernel")), "gbias": put(np.broadcast_to(a("L0_ffn_gate_bias"), (P, E))),
        "wq": put(a("L0_attn_Wq").T), "wk": put(a("L0_attn_Wk").T), "wv": put(a("L0_attn_Wv").T),
        "wf": put(np.concatenate([a("L0_attn_Wf").T.reshape(2, P // 2, D).transpose(1, 0, 2),
                                  np.stack([a("L0_attn_bf"), np.zeros_like(a("L0_attn_bf"))])[None]], 0)),
        "ident_in": np.eye(P, dtype=np.float32), "mask_in": put(mask), "sel_in": sel, "tri_in": put(tri),
        "beta_in": put(beta),
    }
    nc = bacc.Bacc("TRN2", target_bir_lowering=False, num_devices=1)
    args = [nc.dram_tensor(n, z.shape, mybir.dt.from_np(z.dtype), kind="ExternalInput").ap()
            for n, z in arrays.items()]
    out = nc.dram_tensor("out", (NB * SEQ, D), F32, kind="ExternalOutput").ap()
    macaron(nc, *args, out)
    r = run_bass_kernel_spmd(nc, [arrays], core_ids=[0])
    return r.results[0]["out"].reshape(NB, SEQ, D)
```
